# Optimizing a Trainium2 kernel written in Bass

```python
import numpy as np
import jax
import jax.numpy as jnp

def _softmax(x, axis=-1):
    return jax.nn.softmax(x, axis=axis)

def _gelu(x):
    return jax.nn.gelu(x, approximate=True)

def _silu(x):
    return jax.nn.silu(x)

def _sigmoid(x):
    return jax.nn.sigmoid(x)

def _layernorm(x, axis=-1, eps=1e-05):
    m = jnp.mean(x, axis=axis, keepdims=True)
    v = jnp.var(x, axis=axis, keepdims=True)
    return (x - m) / jnp.sqrt(v + eps)

def _scatter_add(tgt, idx, src, axis=0):
    return tgt.at[idx].add(src)

def _segment_sum(src, seg, n):
    return jax.ops.segment_sum(src, seg, n)
kernel_name = 'mk_sandwich_d1_jaxref_r4_399ae6'

def setup_inputs(seed: int=0):
    np.random.seed(seed)
    _w = jnp.asarray

    def _L0_attn_setup():
        import jax, jax.numpy as jnp
        import numpy as np
        B, S, D = (2, 512, 1024)
        NH, NKV = (32, 8)
        HD = D // NH
        NREP = NH // NKV
        SCALE = HD ** (-0.5)
        key = jax.random.key(seed)
        kx, kq, kk, kv, ko = jax.random.split(key, 5)
        s = 0.02
        return {'x': jax.random.normal(kx, (B, S, D), dtype=jnp.float32), 'wq': jax.random.normal(kq, (D, NH * HD), dtype=jnp.float32) * s, 'wk': jax.random.normal(kk, (D, NKV * HD), dtype=jnp.float32) * s, 'wv': jax.random.normal(kv, (D, NKV * HD), dtype=jnp.float32) * s, 'wo': jax.random.normal(ko, (NH * HD, D), dtype=jnp.float32) * s}
    _L0_attn_in = _L0_attn_setup()

    def _L0_ffn_setup():
        import jax, jax.numpy as jnp
        import numpy as np
        H = 1024
        I = 3584
        G = 128

        def dequant(q, s, g=G):
            O, In = q.shape
            return (q.reshape(O, In // g, g).astype(s.dtype) * s[:, :, None]).reshape(O, In)
        key = jax.random.key(seed)
        ks = jax.random.split(key, 7)
        x = jax.random.normal(ks[0], (2, 512, H), dtype=jnp.float32)

        def mk_qlinear(kq, ksc, out_d, in_d):
            q = jax.random.randint(kq, (out_d, in_d), -8, 8, dtype=jnp.int32)
            s = jax.random.uniform(ksc, (out_d, in_d // G), dtype=jnp.float32, minval=0.005, maxval=0.02)
            return (q, s)
        gate_q, gate_s = mk_qlinear(ks[1], ks[2], I, H)
        up_q, up_s = mk_qlinear(ks[3], ks[4], I, H)
        down_q, down_s = mk_qlinear(ks[5], ks[6], H, I)
        return {'x': x, 'gate_q': gate_q, 'gate_s': gate_s, 'up_q': up_q, 'up_s': up_s, 'down_q': down_q, 'down_s': down_s}
    _L0_ffn_in = _L0_ffn_setup()
    _d = {'L0_attn_x': _L0_attn_in['x'], 'L0_attn_wq': _L0_attn_in['wq'], 'L0_attn_wk': _L0_attn_in['wk'], 'L0_attn_wv': _L0_attn_in['wv'], 'L0_attn_wo': _L0_attn_in['wo'], 'L0_ffn_gate_q': _L0_ffn_in['gate_q'], 'L0_ffn_gate_s': _L0_ffn_in['gate_s'], 'L0_ffn_up_q': _L0_ffn_in['up_q'], 'L0_ffn_up_s': _L0_ffn_in['up_s'], 'L0_ffn_down_q': _L0_ffn_in['down_q'], 'L0_ffn_down_s': _L0_ffn_in['down_s']}
    _x0 = _d['L0_attn_x']
    _d['L0_attn_x'] = jax.random.normal(jax.random.fold_in(jax.random.key(seed), 1), (4, 512, 1024), dtype=_x0.dtype)
    del _x0
    return _d

def reference(L0_attn_x, L0_attn_wq, L0_attn_wk, L0_attn_wv, L0_attn_wo, L0_ffn_gate_q, L0_ffn_gate_s, L0_ffn_up_q, L0_ffn_up_s, L0_ffn_down_q, L0_ffn_down_s):

    def _L0_attn_ref(x, wq, wk, wv, wo):
        import jax, jax.numpy as jnp
        import numpy as np
        B, S, D = (2, 512, 1024)
        NH, NKV = (32, 8)
        HD = D // NH
        NREP = NH // NKV
        SCALE = HD ** (-0.5)
        b, s, _ = x.shape
        q = (x @ wq).reshape(b, s, NH, HD)
        k = (x @ wk).reshape(b, s, NKV, HD)
        v = (x @ wv).reshape(b, s, NKV, HD)
        k = jnp.repeat(k, NREP, axis=2)
        v = jnp.repeat(v, NREP, axis=2)
        scores = jnp.einsum('bihd,bjhd->bhij', q, k) * SCALE
        causal = jnp.tril(jnp.ones((s, s), dtype=bool))
        scores = jnp.where(causal, scores, jnp.finfo(scores.dtype).min)
        attn = jax.nn.softmax(scores, axis=-1)
        out = jnp.einsum('bhij,bjhd->bihd', attn, v)
        out = out.reshape(b, s, NH * HD)
        return out @ wo

    def _L0_ffn_ref(x, gate_q, gate_s, up_q, up_s, down_q, down_s):
        import jax, jax.numpy as jnp
        import numpy as np
        H = 1024
        I = 3584
        G = 128

        def dequant(q, s, g=G):
            O, In = q.shape
            return (q.reshape(O, In // g, g).astype(s.dtype) * s[:, :, None]).reshape(O, In)
        Wg = dequant(gate_q, gate_s)
        Wu = dequant(up_q, up_s)
        Wd = dequant(down_q, down_s)
        gate_score = jax.nn.silu(jnp.einsum('bsh,ih->bsi', x, Wg))
        intermediate = gate_score * jnp.einsum('bsh,ih->bsi', x, Wu)
        return jnp.einsum('bsi,hi->bsh', intermediate, Wd)
    x = L0_attn_x
    x = x + _layernorm(_L0_attn_ref(_layernorm(x, axis=-1), L0_attn_wq, L0_attn_wk, L0_attn_wv, L0_attn_wo), axis=-1)
    x = x + _layernorm(_L0_ffn_ref(_layernorm(x, axis=-1), L0_ffn_gate_q, L0_ffn_gate_s, L0_ffn_up_q, L0_ffn_up_s, L0_ffn_down_q, L0_ffn_down_s), axis=-1)
    return x

_drawn_inputs = setup_inputs


def setup_inputs(seed=0):
    import zlib

    import numpy as np

    out = dict(_drawn_inputs(seed))
    spreads = {}
    factors = {}
    for name, (base, spread) in spreads.items():
        noise = np.random.default_rng([zlib.crc32(name.encode()), seed]).standard_normal(out[name].shape)
        drawn = base * np.exp(spread * noise) if base else spread * noise
        out[name] = jnp.asarray(drawn.astype(out[name].dtype))
    for name, factor in factors.items():
        out[name] = (out[name] * factor).astype(out[name].dtype)
    return out
```

```python
from contextlib import ExitStack

import concourse.bass as bass
from concourse import mybir

F32 = mybir.dt.float32
F16 = mybir.dt.float16
BF16 = mybir.dt.bfloat16
I32 = mybir.dt.int32
ALU = mybir.AluOpType
ACT = mybir.ActivationFunctionType
AX = mybir.AxisListType

P = 128
HD = 32
SOFTMAX_ROWS = 98
MAX_UNIT = 32768.0


def sandwich(nc, x, wq, wk, wv, wo, gu_t, down_t, scales, out):
    NB, S, D = x.shape
    NH = wq.shape[1] // HD
    NKV = wk.shape[1] // HD
    NREP = NH // NKV
    KD = D // P
    TT = S // P
    NT = gu_t.shape[0]
    NTOK = NB * S
    HALF = 2 * S
    NU = NH // 8
    EPS = 1e-5
    assert HD * NREP == P and KD == 8 and TT == 4 and S == 512 and NB == 4 and NKV == 8

    x1_scr = nc.dram_tensor("x1_scratch", [NB, TT, P, D], F32, kind="Internal").ap()
    xt_scr = nc.dram_tensor("xt_scratch", [NB, P, 2 * KD * S], F16, kind="Internal").ap()

    NEG = -1.0e30
    KOFF = [0, 512, 1024, 896]
    KLEN = [S - P * j for j in range(TT)]
    TRI = 1280

    with ExitStack() as ctx:
        ARENA = 53200
        arena = ctx.enter_context(nc.sbuf_tensor("arena", [P, ARENA], F32))
        place = {"at": 0}

        def carve(words, dtype=F32, at=None):
            if at is None:
                at = place["at"]
                place["at"] = at + words
                assert place["at"] <= ARENA, place["at"]
            v = arena[:, at:at + words]
            return v if dtype == F32 else v.bitcast(dtype)

        ident = carve(P)
        all_scales = carve(NT * 25).rearrange("p (n c) -> p n c", n=NT)
        gu_sc = carve(2 * 25).rearrange("p (b c) -> p b c", b=2)
        dn_sc = carve(2 * 8).rearrange("p (b c) -> p b c", b=2)
        neg_half = carve(1)
        wabs = carve(4)
        wall = carve(4)
        wpow = carve(4)
        wfac = carve(4)
        score_f = carve(1)
        out_f = carve(1)
        stats = carve(2 * 12).rearrange("p (b c) -> p b c", b=2)
        mv = carve(2 * 2).rearrange("p (b c) -> p b c", b=2)
        vpe = carve(2)
        rstd = carve(2)
        rs2 = carve(2)
        rsum = carve(2 * TT).rearrange("p (b t d) -> p b t d", b=2, d=1)
        base = place["at"]

        w_q = carve(8192, F16).rearrange("p (s k n) -> p s k n", s=2, k=KD)
        w_k = carve(2048, F16).rearrange("p (s k n) -> p s k n", s=2, k=KD)
        w_v = carve(2048, F16).rearrange("p (s k n) -> p s k n", s=2, k=KD)
        w_o = carve(8192, F16).rearrange("p (s k n) -> p s k n", s=2, k=KD)
        xin = carve(2 * D).rearrange("p (b n) -> p b n", b=2)
        xnt = carve(4096, F16).rearrange("p (s k n) -> p s k n", s=2, k=KD)
        at_t = xnt
        qt_at = place["at"]
        qt = carve(2048, F16).rearrange("p (s b m n) -> p s b m n", s=2, b=2, m=2)
        qs_at = place["at"]
        q_s = carve(8192, F16).rearrange("p (h n) -> p h n", h=NH)
        k_s = carve(2048, F16).rearrange("p (g n) -> p g n", g=NKV)
        v_a = carve(TT * NKV * 33 // 2, F16).rearrange("p (t g d) -> p t g d", t=TT, g=NKV)
        v_b = carve(TT * NKV * 33 // 2, F16).rearrange("p (t g d) -> p t g d", t=TT, g=NKV)
        p_at = place["at"]
        p32 = carve(2 * TRI).rearrange("p (b n) -> p b n", b=2)
        p_hl = carve(2 * TRI, F16).rearrange("p (b s n) -> p b s n", b=2, s=2)
        attn = carve(TT * D).rearrange("p (t n) -> p t n", t=TT)
        xr_at = place["at"]
        xr = carve(2 * D).rearrange("p (b n) -> p b n", b=2)
        mask = carve(S // 2, BF16)
        mcol = carve(NU * TT * 8).rearrange("p (u t h) -> p u t h", u=NU, t=TT)
        mrow = carve(S, F16).rearrange("p (s n) -> p s n", s=2)
        stage_q = carve(8192, at=qs_at).rearrange("p (k n) -> p k n", k=KD)
        stage_o = carve(8192, at=p_at).rearrange("p (k n) -> p k n", k=KD)
        stage_k = carve(2048, at=xr_at).rearrange("p (k n) -> p k n", k=KD)
        stage_v = carve(2048, at=qt_at).rearrange("p (k n) -> p k n", k=KD)
        x2t = carve(4096, F16, at=qs_at).rearrange("p (s k n) -> p s k n", s=2, k=KD)
        x2t_flat = carve(4096, F16, at=qs_at)
        x1 = carve(2 * D, at=qs_at + 4096).rearrange("p (b n) -> p b n", b=2)
        xn2 = carve(2 * D, at=qs_at + 4096 + 2 * D).rearrange("p (b n) -> p b n", b=2)

        place["at"] = base
        xt = carve(NB * 4096, F16).rearrange("p (b s k n) -> p b s k n", b=NB, s=2, k=KD)
        xt_flat = carve(NB * 4096, F16, at=base).rearrange("p (b n) -> p b n", b=NB)
        acc = carve(KD * NTOK).rearrange("p (o n) -> p o n", o=KD)
        gacc = carve(2 * NTOK).rearrange("p (b n) -> p b n", b=2)
        uacc = carve(NTOK)
        hid = carve(2 * NTOK, F16).rearrange("p (b s n) -> p b s n", b=2, s=2)
        RT = 3
        tmp = carve(RT * HALF).rearrange("p (r n) -> p r n", r=RT)
        int_gu = carve(2 * KD * P, I32)
        int_d = carve(D, I32)
        w_gu = carve(2 * KD * P, BF16).rearrange("p (b w k n) -> p b w k n", b=2, w=2, k=KD)
        w_d = carve(D, BF16).rearrange("p (b n) -> p b n", b=2)
        y_t = carve(4 * D, at=base).rearrange("p (b n) -> p b n", b=4)
        x1_b = carve(4 * D, at=base + 4 * D).rearrange("p (b n) -> p b n", b=4)

        psum = ctx.enter_context(nc.psum_tensor("psum", [P, 8 * 512], F32))
        job_slot = [psum[:, 0:1536], psum[:, 1536:3072]]
        pv_ps = [psum[:, 3072:3204], psum[:, 3584:3716]]
        ffn_slot = [psum[:, 1024 * s:1024 * s + 1024] for s in range(4)]

        def sem(name):
            return ctx.enter_context(nc.semaphore(name))

        ident_ready = sem("ident_ready")
        consts_ready = sem("consts_ready")
        settled = sem("settled")
        x_loaded = [sem(f"x_loaded{i}") for i in range(2)]
        w_loaded = [sem(f"w_loaded{i}") for i in range(4)]
        s_loaded = sem("s_loaded")
        wabs_ready = sem("wabs_ready")
        wall_ready = sem("wall_ready")
        wfac_ready = sem("wfac_ready")
        whi_ready = sem("whi_ready")
        wlo_ready = sem("wlo_ready")
        dve_step = sem("dve_step")
        scales_ready = sem("scales_ready")
        var_ready = sem("var_ready")
        rstd_ready = sem("rstd_ready")
        xn_ready = sem("xn_ready")
        slot_full = [sem(f"slot_full{i}") for i in range(2)]
        slot_free = [sem(f"slot_free{i}") for i in range(2)]
        hi_ready = sem("hi_ready")
        ks_stacked = sem("ks_stacked")
        qs_stacked = [sem(f"qs_stacked{i}") for i in range(2)]
        mhi_ready = sem("mhi_ready")
        mrow_loaded = sem("mrow_loaded")
        p_masked = sem("p_masked")
        phi_ready = sem("phi_ready")
        plo_ready = sem("plo_ready")
        pv_full = sem("pv_full")
        pv_free = sem("pv_free")
        xr_loaded = [sem(f"xr_loaded{i}") for i in range(2)]
        x1_ready = sem("x1_ready")
        x1_stored = [sem(f"x1_stored{i}") for i in range(2)]
        x2t_stored = sem("x2t_stored")
        xt_loaded = [sem(f"xt_loaded{b}") for b in range(NB)]
        acc_zero = sem("acc_zero")
        unit_full = [sem(f"unit_full{s}") for s in range(4)]
        unit_free = [sem(f"unit_free{s}") for s in range(4)]
        gu_loaded = sem("gu_loaded")
        d_loaded = sem("d_loaded")
        gu_conv = sem("gu_conv")
        d_conv = sem("d_conv")
        gusc_ready = sem("gusc_ready")
        dnsc_ready = sem("dnsc_ready")
        silu_done = sem("silu_done")
        h32_ready = sem("h32_ready")
        hhi_ready = sem("hhi_ready")
        h_ready = sem("h_ready")
        tmp_free = sem("tmp_free")
        fvar_ready = sem("fvar_ready")
        frstd_ready = sem("frstd_ready")
        fnmr_ready = sem("fnmr_ready")
        x1b_loaded = [sem(f"x1b_loaded{i}") for i in range(4)]
        out_ready = sem("out_ready")
        out_stored = [sem(f"out_stored{i}") for i in range(4)]

        def settle(eng):
            eng.sem_inc(settled, 1)

        def wait(eng, s, value):
            if not isinstance(value, int):
                eng.wait_ge(s, value)
                if eng is nc.sync:
                    settle(eng)
            elif value > 0:
                eng.wait_ge(s, value)

        LEAD = 12
        events = [("T1", t) for t in range(TT)] + [("K", 0), ("K", 1), ("V", 0), ("V", 1)]
        events += [("Q", m) for m in range(4)]
        for m in range(4, 8):
            events += [("M", h) for h in range(3 * (m - 4), 3 * (m - 4) + 3)] + [("Q", m)]
        events += [("MT", 0)]
        for h in range(NH):
            events += [("S", h)]
            if h + LEAD < NH:
                events += [("M", h + LEAD)]
            if h >= 2:
                events += [("PV", h - 2)]
            if h % 8 == 5 and h < NH - 8:
                events += [("MT", h // 8 + 1)]
        events += [("END", 0), ("PV", NH - 2), ("PV", NH - 1)]
        events += [("T2", 0), ("T2", 1), ("WO", 0), ("T2", 2), ("WO", 1), ("T2", 3), ("WO", 2), ("T3", 0),
                   ("WO", 3), ("T3", 1), ("T3", 2), ("T3", 3)]
        jobs = [e for e in events if e[0] not in ("PV", "END")]
        J = {job: n for n, job in enumerate(jobs)}
        NJ = len(jobs)
        assert NJ % 2 == 0

        def slot(job):
            return job_slot[J[job] % 2]

        def wait_full(eng, b, job):
            wait(eng, slot_full[J[job] % 2], b * (NJ // 2) + J[job] // 2 + 1)

        def wait_free(eng, b, job):
            wait(eng, slot_free[J[job] % 2], b * (NJ // 2) + J[job] // 2 + 1)

        def full(ins, job):
            ins.then_inc(slot_full[J[job] % 2], 1)

        def free(ins, job):
            ins.then_inc(slot_free[J[job] % 2], 1)

        SPLIT = ("T1", "K", "V", "Q", "T2", "T3")
        split_jobs = [j for j in jobs if j[0] in SPLIT]
        HI = {j: n for n, j in enumerate(split_jobs)}
        NHI = len(split_jobs)

        def split_views(job):
            kind, i = job
            ps = slot(job)
            if kind in ("T1", "T2", "T3"):
                dst = {"T1": xnt, "T2": at_t, "T3": x2t}[kind]
                src = ps[:, 0:1024].rearrange("p (k n) -> p k n", k=KD)
                return src, dst[:, 0, :, P * i:P * i + P], dst[:, 1, :, P * i:P * i + P]
            if kind == "K":
                return ps[:, 0:S], qt[:, 0, 1, i, :], qt[:, 1, 1, i, :]
            if kind == "Q":
                u = i // 2
                return ps[:, 0:S], qt[:, 0, u % 2, i % 2, :], qt[:, 1, u % 2, i % 2, :]
            src = ps[:, 0:S].rearrange("p (t g d) -> p t g d", t=2, g=NKV)
            return src, v_a[:, 2 * i:2 * i + 2, :, 0:HD], v_b[:, 2 * i:2 * i + 2, :, 0:HD]

        MOFF = [896, 1024, 512, 0]

        GU = 4 * KD
        DN = 2 * KD
        AT_H, AT_HI, AT_LO = [1, 2], [3, 4], [5, 7]
        CARRY = 4
        order_zero = [("g", j) for j in range(GU)]
        order, n_d = [], 0
        for j in range(GU):
            order.append(("g", j))
            if j % 2 and j < 2 * CARRY:
                order.append(("c", DN - CARRY + j // 2))
            while n_d < (DN - CARRY) * (j - 2 * CARRY - 1) // (GU - 2 * CARRY - 2):
                order.append(("d", n_d))
                n_d += 1
        assert n_d == DN - CARRY
        order_one = [u for u in order if u[0] != "c"]
        order_last = [("c", j) for j in range(DN - CARRY, DN)] + [("d", 2 * (j % KD) + j // KD) for j in range(DN)]
        DVE_D = [9]
        NPD = DN - len(DVE_D)
        NPC = len([j for j in range(DN - CARRY, DN) if j not in DVE_D])
        assert NPD % RT == 0 and (GU + DN) % 4 == 0 and GU % 4 == 0 and CARRY % 4 == 0

        def unit_list(n):
            if isinstance(n, int) and n < 2:
                units, before = (order_zero, 0) if n == 0 else (order_one, GU // 4)
            else:
                units = order_last if isinstance(n, int) and n == NT else order
                before = n * ((GU + DN) // 4) - (DN + CARRY) // 4
            return {u: (pos % 4, before + pos // 4) for pos, u in enumerate(units)}

        def pool_units(n):
            us = [u for u in unit_list(n) if u[0] != "g" and u[1] not in DVE_D]
            at = 0 if isinstance(n, int) and n == 1 else (n - 1) * NPD - NPC
            return [(u, at + q, (q - (0 if isinstance(n, int) and n == 1 else NPC)) % RT) for q, u in enumerate(us)]

        def gu_parts(j):
            return j // 16, (j % 16) // 2, j % 2

        def unit_done(eng, units, u):
            s, c = units[u]
            eng.wait_ge(unit_free[s], c + 1)

        def unit_filled(eng, units, u):
            s, c = units[u]
            wait(eng, unit_full[s], c + 1)

        def over_tiles(eng, one_tile):
            one_tile(0, 0)
            one_tile(1, 1)
            with eng.Fori(0, (NT - 4) // 2) as i:
                one_tile(i * 2 + 2, 0)
                one_tile(i * 2 + 3, 1)
            one_tile(NT - 2, 0)
            one_tile(NT - 1, 1)

        def over_batches(eng, one_batch):
            one_batch(0)
            with eng.Fori(1, NB - 1) as b:
                one_batch(b)
            one_batch(NB - 1)

        def is_first(b):
            return isinstance(b, int) and b == 0

        def is_last(b):
            return isinstance(b, int) and b == NB - 1

        NF = NTOK // P
        F0 = NT * (GU + DN) // 4

        block = ctx.enter_context(nc.Block())

        @block.sync
        def _(sp):
            x_tiles = x.rearrange("b (t p) n -> b t p n", p=P)

            def load_x23(b):
                for t in range(2, TT):
                    wait_full(sp, b, ("T1", t - 2))
                    sp.dma_start(xin[:, t % 2, :], x_tiles[b, t]).then_inc(x_loaded[t % 2], 16)

            sp.dma_start(xin[:, 0, :], x_tiles[0, 0]).then_inc(x_loaded[0], 16)
            sp.dma_start(xin[:, 1, :], x_tiles[0, 1]).then_inc(x_loaded[1], 16)
            for n, (dst, src) in enumerate(((stage_k, wk), (stage_v, wv), (stage_q, wq), (stage_o, wo))):
                sp.dma_start(dst, src.rearrange("(k p) n -> p k n", p=P)).then_inc(w_loaded[n], 16)
                if n == 1:
                    load_x23(0)
            sp.dma_start(all_scales[:, :, 0:24], scales.rearrange("n p c -> p n c")).then_inc(s_loaded, 16)

            def stack_queries(b, u):
                if u == 0:
                    if is_first(b):
                        wait(sp, wlo_ready, 3)
                    else:
                        for i in range(2):
                            wait(sp, x1_stored[i], b * 32)
                        wait(sp, x2t_stored, b * 16)
                wait_free(sp, b, ("Q", 2 * u))
                wait_free(sp, b, ("Q", 2 * u + 1))
                for c in range(3):
                    rows = q_s[HD * c:HD * c + HD, 8 * u:8 * u + 8, :].rearrange("p (m r) n -> p m r n", r=NREP)
                    for r in range(NREP):
                        sp.dma_start(rows[:, :, r, :], qt[HD * r:HD * r + HD, 1 if c == 1 else 0, u % 2, :, :])\
                            .then_inc(qs_stacked[u % 2], 16)

            def send_max(b, u):
                wait_free(sp, b, ("MT", u))
                for s in range(2):
                    sp.dma_start(q_s[3 * HD + s:3 * HD + s + 1, 8 * u:8 * u + 8, :],
                                 mrow[0:8, s, :]).then_inc(mrow_loaded, 16)

            def batch(b):
                if not is_first(b):
                    load_x23(b)
                wait_free(sp, b, ("K", 0))
                wait_free(sp, b, ("K", 1))
                for c in range(3):
                    rows = k_s[HD * c:HD * c + HD, :, :].rearrange("p (m r) n -> p m r n", r=NREP)
                    for r in range(NREP):
                        sp.dma_start(rows[:, :, r, :], qt[HD * r:HD * r + HD, 1 if c == 2 else 0, 1, :, :])\
                            .then_inc(ks_stacked, 16)
                stack_queries(b, 0)
                stack_queries(b, 1)
                stack_queries(b, 2)
                stack_queries(b, 3)
                for u in range(NU):
                    send_max(b, u)
                if not is_last(b):
                    for t in range(2):
                        wait_full(sp, b, ("T1", t + 2))
                        sp.dma_start(xin[:, t, :], x_tiles[b + 1, t]).then_inc(x_loaded[t], 16)
                else:
                    wait_full(sp, b, ("Q", 6))
                    wait_full(sp, b, ("Q", 7))
                    for i in range(NB - 1):
                        sp.dma_start(xt_flat[:, i, :], xt_scr[i]).then_inc(xt_loaded[i], 16)
                for t in range(TT):
                    if t >= 2:
                        wait(sp, x1_ready, b * TT + t - 1)
                    elif is_first(b):
                        wait(sp, wlo_ready, 4)
                    else:
                        wait(sp, x1_ready, b * TT)
                    sp.dma_start(xr[:, t % 2, :], x_tiles[b, t]).then_inc(xr_loaded[t % 2], 16)
                    if t >= 2:
                        sp.dma_start(x1_scr[b, t - 2], x1[:, t % 2, :]).then_inc(x1_stored[t % 2], 16)
                for t in range(2, TT):
                    wait(sp, x1_ready, b * TT + t + 1)
                    sp.dma_start(x1_scr[b, t], x1[:, t % 2, :]).then_inc(x1_stored[t % 2], 16)
                if is_last(b):
                    wait_full(sp, b, ("T2", 3))
                    sp.dma_start(int_gu, gu_t[0]).then_inc(gu_loaded, 16)
                wait_free(sp, b, ("T3", 2))
                wait_free(sp, b, ("T3", 3))
                sp.dma_start(xt_scr[b], x2t_flat).then_inc(x2t_stored, 16)

            over_batches(sp, batch)
            wait(sp, x2t_stored, 16 * NB)
            sp.dma_start(xt_flat[:, NB - 1, :], xt_scr[NB - 1]).then_inc(xt_loaded[NB - 1], 16)
            sp.dma_start(int_d, down_t[0]).then_inc(d_loaded, 16)

            def tile(n, par):
                if isinstance(n, int) and n == NT - 1:
                    return
                wait(sp, gu_conv, n + 1)
                sp.dma_start(int_gu, gu_t[n + 1]).then_inc(gu_loaded, 16)
                wait(sp, d_conv, n + 1)
                sp.dma_start(int_d, down_t[n + 1]).then_inc(d_loaded, 16)

            over_tiles(sp, tile)

            last = unit_list(NT - 1)
            for u in order[-4:]:
                unit_filled(sp, last, u)
            for f in range(NF + 2):
                if f < NF:
                    if f >= 4:
                        wait(sp, out_ready, f - 3)
                    sp.dma_start(x1_b[:, f % 4, :], x1_scr[f // TT, f % TT]).then_inc(x1b_loaded[f % 4], 16)
                if f >= 2:
                    g = f - 2
                    wait(sp, out_ready, g + 1)
                    sp.dma_start(out[g * P:g * P + P, :], y_t[:, g % 4, :]).then_inc(out_stored[g % 4], 16)
            for i in range(4):
                wait(sp, out_stored[i], 16 * NF // 4)

        @block.gpsimd
        def _(pool):
            pool.memset(ident, 0.0).then_inc(ident_ready, 1)
            pool.wait_ge(ident_ready, 1)
            pool.affine_select(out=ident, in_=ident, compare_op=ALU.not_equal, fill=1.0, base=0,
                               pattern=[[-1, P]], channel_multiplier=1).then_inc(ident_ready, 1)
            pool.memset(neg_half, -0.5).then_inc(consts_ready, 1)
            pool.memset(mask, 0.0).then_inc(consts_ready, 1)
            pool.wait_ge(consts_ready, 2)
            tri = mask[:, S - P:S]
            pool.affine_select(out=tri, in_=tri, compare_op=ALU.is_ge, fill=NEG, base=0,
                               pattern=[[-1, P]], channel_multiplier=1).then_inc(consts_ready, 1)
            pool.memset(v_a.rearrange("p t g d -> p (t g d)"), 1.0).then_inc(consts_ready, 1)
            pool.memset(v_b.rearrange("p t g d -> p (t g d)"), 0.0).then_inc(consts_ready, 1)
            pool.wait_ge(consts_ready, 5)
            pool.memset(k_s[3 * HD:SOFTMAX_ROWS, :, :].rearrange("p g n -> p (g n)"), MAX_UNIT).then_inc(consts_ready, 1)
            pool.wait_ge(consts_ready, 6)

            def power(count, i):
                pool.wait_ge(var_ready, count)
                pool.tensor_tensor(rstd[:, i:i + 1], vpe[:, i:i + 1], neg_half, ALU.pow).then_inc(rstd_ready, 1)

            def weight_max(n):
                pool.wait_ge(wabs_ready, n + 1)
                pool.partition_all_reduce(wall[:, n:n + 1], wabs[:, n:n + 1], P,
                                          bass.bass_isa.ReduceOp.max).then_inc(wall_ready, 1)

            def batch(b):
                for t in range(TT):
                    power(b * 3 * TT + t + 1, t % 2)
                    if is_first(b) and t < 2:
                        weight_max(t)
                if is_first(b):
                    weight_max(2)
                    weight_max(3)
                for h in range(NH):
                    wait_free(pool, b, ("S", h))
                    settle(pool)
                    for j in range(TT):
                        d = p32[:, h % 2, KOFF[j]:KOFF[j] + P]
                        ins = pool.affine_select(out=d, in_=d, compare_op=ALU.is_ge, fill=0.0, base=0,
                                                 pattern=[[1, P]], channel_multiplier=-1)
                    ins.then_inc(p_masked, 1)
                for t in range(TT):
                    for i in range(2):
                        power(b * 3 * TT + TT + 2 * t + i + 1, i)

            over_batches(pool, batch)
            pool.sem_inc(tmp_free, RT)
            pool.wait_ge(x2t_stored, 16 * NB)
            pool.memset(acc.rearrange("p o n -> p (o n)"), 0.0).then_inc(acc_zero, 1)
            pool.wait_ge(acc_zero, 1)

            def tile(n, par):
                units = unit_list(n)
                for u, number, buf in pool_units(n):
                    o, c = u[1] // 2, u[1] % 2
                    unit_done(pool, units, u)
                    pool.wait_ge(tmp_free, RT + number - 1)
                    a = acc[:, o, c * HALF:c * HALF + HALF]
                    pool.tensor_tensor(a, tmp[:, buf, :], a, ALU.add).then_inc(tmp_free, 1)

            over_tiles(pool, tile)
            tile(NT, 0)
            for f in range(NF):
                pool.wait_ge(fvar_ready, f + 1)
                pool.tensor_tensor(rstd[:, f % 2:f % 2 + 1], vpe[:, f % 2:f % 2 + 1], neg_half,
                                   ALU.pow).then_inc(frstd_ready, 1)

        @block.scalar
        def _(act):
            w_hi = [w_k[:, 0], w_v[:, 0], w_q[:, 0], w_o[:, 0]]
            stages = [stage_k, stage_v, stage_q, stage_o]

            def weight_hi(n):
                act.wait_ge(wfac_ready, n + 1)
                act.activation(w_hi[n], stages[n], ACT.Copy, scale=wfac[:, n:n + 1]).then_inc(whi_ready, 1)

            def probabilities_hi(b, h):
                act.wait_ge(p_masked, b * NH + h + 1)
                wait(act, pv_full, b * NH + h - 1)
                act.activation(p_hl[:, h % 2, 0, :], p32[:, h % 2, :], ACT.Copy).then_inc(phi_ready, 1)

            def batch(b):
                for ev in events:
                    kind, i = ev
                    if kind in SPLIT:
                        if is_first(b) and ev == ("T1", 0):
                            weight_hi(0)
                            weight_hi(1)
                        if is_first(b) and ev == ("Q", 0):
                            weight_hi(2)
                        if kind == "K":
                            if i == 0:
                                sp_waits_qt(act, b, 1)
                        elif kind == "Q" and i % 2 == 0:
                            sp_waits_qt(act, b, 2 + i // 2)
                        elif ev == ("V", 0):
                            if is_first(b):
                                act.wait_ge(consts_ready, 6)
                        elif ev == ("T3", 0):
                            pass
                        wait_full(act, b, ev)
                        src, hi, _ = split_views(ev)
                        act.activation(hi, src, ACT.Copy).then_inc(hi_ready, 1)
                    elif kind == "S":
                        if is_first(b) and i == 0:
                            weight_hi(3)
                            act.wait_ge(wlo_ready, 4)
                            act.wait_ge(scales_ready, 1)
                        wait_full(act, b, ev)
                        wait(act, plo_ready, b * NH + i - 1)
                        free(act.activation(p32[:, i % 2, :], slot(ev)[:, 0:TRI], ACT.Exp,
                                            scale=score_f[:, 0:1]), ev)
                        if i >= 1:
                            probabilities_hi(b, i - 1)
                    elif kind == "END":
                        probabilities_hi(b, NH - 1)
                    elif kind == "MT":
                        wait_full(act, b, ev)
                        wait(act, mrow_loaded, (b * NU + i) * 32)
                        act.activation(mrow[0:8, 0, :], slot(ev)[0:8, 0:S], ACT.Copy,
                                       scale=-1.0 / MAX_UNIT).then_inc(mhi_ready, 1)

            def sp_waits_qt(eng, b, k):
                if k == 1:
                    wait(eng, qs_stacked[1], b * 384)
                    if is_first(b):
                        eng.wait_ge(wlo_ready, 2)
                elif k == 2:
                    wait(eng, qs_stacked[0], b * 384)
                elif k == 3:
                    eng.wait_ge(ks_stacked, (b + 1) * 192)
                else:
                    eng.wait_ge(qs_stacked[k % 2], b * 384 + 192)

            over_batches(act, batch)

            def convert_gu(n, par):
                act.wait_ge(gu_loaded, (n + 1) * 16)
                act.activation(w_gu[:, par].rearrange("p w k n -> p (w k n)"), int_gu, ACT.Copy).then_inc(gu_conv, 1)

            def convert_d(n, par):
                act.wait_ge(d_loaded, (n + 1) * 16)
                act.wait_ge(gusc_ready, n + 1)
                act.activation(w_d[:, par, :], int_d, ACT.Copy, scale=gu_sc[:, par, 24:25]).then_inc(d_conv, 1)

            convert_gu(0, 0)

            def down_unit(par, units, u, number, buf):
                o = u[1] // 2
                unit_filled(act, units, u)
                act.wait_ge(tmp_free, number + 1)
                act.activation(tmp[:, buf, :], ffn_slot[units[u][0]], ACT.Copy,
                               scale=dn_sc[:, par if u[0] == "c" else 1 - par, o:o + 1])\
                    .then_inc(unit_free[units[u][0]], 1)

            def tile(n, par):
                units = unit_list(n)
                down = {u: (number, buf) for u, number, buf in pool_units(n)}
                seen_d = False
                for u in units:
                    kind, j = u
                    if kind == "g":
                        w, g, c = gu_parts(j)
                        if j in AT_HI and not (isinstance(n, int) and n == 0):
                            hidden_hi(n - 1, 1 - par, AT_HI.index(j))
                        if g == 0:
                            unit_filled(act, units, u)
                            act.wait_ge(gusc_ready, n + 1)
                            if w == 0:
                                dst = gacc[:, par, c * HALF:c * HALF + HALF]
                            else:
                                wait(act, h_ready, n * 2)
                                dst = uacc[:, c * HALF:c * HALF + HALF]
                            act.activation(dst, ffn_slot[units[u][0]], ACT.Copy,
                                           scale=gu_sc[:, par, 8 * w:8 * w + 1]).then_inc(unit_free[units[u][0]], 1)
                        if j in (20, 21):
                            unit_done(act, units, ("g", j - 6))
                            ga = gacc[:, par, (j - 20) * HALF:(j - 20) * HALF + HALF]
                            act.activation(ga, ga, ACT.Silu).then_inc(silu_done, 1)
                        if j == 10:
                            if ("c", DN - 1) in units:
                                unit_filled(act, units, ("c", DN - 1))
                            convert_d(n, par)
                        if j == 25 and not (isinstance(n, int) and n == NT - 1):
                            convert_gu(n + 1, 1 - par)
                    elif u in down:
                        if kind == "d" and not seen_d:
                            act.wait_ge(dnsc_ready, n)
                            seen_d = True
                        down_unit(par, units, u, *down[u])

            def hidden_hi(m, par, c):
                act.wait_ge(h32_ready, m * 2 + c + 1)
                act.activation(hid[:, par, 0, c * HALF:c * HALF + HALF], uacc[:, c * HALF:c * HALF + HALF],
                               ACT.Copy).then_inc(hhi_ready, 1)

            over_tiles(act, tile)
            units = unit_list(NT)
            for c in range(2):
                hidden_hi(NT - 1, 1, c)
            act.wait_ge(dnsc_ready, NT)
            for u, number, buf in pool_units(NT):
                down_unit(0, units, u, number, buf)
            for f in range(NF):
                act.wait_ge(fnmr_ready, f + 1)
                if f >= 4:
                    act.wait_ge(out_stored[f % 4], 16 * (f // 4))
                act.activation(y_t[:, f % 4, :], ffn_slot[f % 4], ACT.Identity, bias=rs2[:, f % 2:f % 2 + 1],
                               scale=rstd[:, f % 2:f % 2 + 1]).then_inc(unit_free[f % 4], 1)

        @block.vector
        def _(dve):
            steps = {"base": 0, "n": 0}

            def link(ins):
                ins.then_inc(dve_step, 1)
                steps["n"] += 1
                dve.wait_ge(dve_step, steps["base"] + steps["n"])

            def variance(halves, i, fac=None):
                for k in range(2):
                    ins = dve.bn_stats(stats[:, i, 6 * k:6 * k + 6], halves[k])
                link(ins)
                settle(dve)
                link(dve.bn_aggr(mv[:, i, :], stats[:, i, :]))
                src = mv[:, i, 1:2]
                if fac is not None:
                    link(dve.tensor_scalar(vpe[:, i:i + 1], src, fac, fac, ALU.mult, ALU.mult))
                    src = vpe[:, i:i + 1]
                return dve.tensor_scalar(vpe[:, i:i + 1], src, EPS, None, ALU.add)

            w_stage = [stage_k, stage_v, stage_q, stage_o]
            w_hl = [w_k, w_v, w_q, w_o]

            def weight_factor(n):
                dve.wait_ge(w_loaded[n], 16)
                dve.tensor_reduce(wabs[:, n:n + 1], w_stage[n].rearrange("p k n -> p (k n)"), AX.X, ALU.max,
                                  apply_absolute_value=True).then_inc(wabs_ready, 1)
                dve.wait_ge(wall_ready, n + 1)
                power_of_two(wpow[:, n:n + 1], wall[:, n:n + 1])
                link(dve.tensor_scalar(wall[:, n:n + 1], wpow[:, n:n + 1], 0.5, None, ALU.mult))
                dve.reciprocal(wfac[:, n:n + 1], wall[:, n:n + 1]).then_inc(wfac_ready, 1)

            def power_of_two(dst, src):
                link(dve.tensor_scalar(dst, src, 1e-30, 1e30, ALU.max, ALU.min))
                link(dve.tensor_scalar(dst.bitcast(I32), dst.bitcast(I32), 0x7F800000, None, ALU.bitwise_and))

            def weight_lo(n):
                dve.wait_ge(whi_ready, n + 1)
                flat = "p k n -> p (k n)"
                dve.scalar_tensor_tensor(out=w_hl[n][:, 1].rearrange(flat), in0=w_stage[n].rearrange(flat),
                                         scalar=wfac[:, n:n + 1], in1=w_hl[n][:, 0].rearrange(flat),
                                         op0=ALU.mult, op1=ALU.subtract).then_inc(wlo_ready, 1)

            def scale_tables():
                dve.wait_ge(s_loaded, 16)
                link(dve.tensor_scalar(score_f, wpow[:, 0:1], wpow[:, 2:3], 0.25 * HD ** -0.5, ALU.mult, ALU.mult))
                link(dve.tensor_scalar(out_f, wpow[:, 1:2], wpow[:, 3:4], 0.25, ALU.mult, ALU.mult))
                inv = all_scales[:, :, 24:25]
                dve.wait_ge(wlo_ready, 4)
                low = stage_o[:, 0, 0:NT].rearrange("p (n c) -> p n c", c=1)
                link(dve.tensor_reduce(inv, all_scales[:, :, 0:8], AX.X, ALU.max, apply_absolute_value=True))
                link(dve.tensor_reduce(low, all_scales[:, :, 8:16], AX.X, ALU.max, apply_absolute_value=True))
                link(dve.tensor_tensor(inv, inv, low, ALU.mult))
                power_of_two(inv, inv)
                link(dve.tensor_scalar(inv, inv, 4096.0, None, ALU.mult))
                link(dve.reciprocal(low, inv))
                up = all_scales[:, :, 8:16]
                dve.tensor_tensor(up, up, low.broadcast_to([P, NT, 8]), ALU.mult).then_inc(scales_ready, 1)

            def layer_norm_in(b, t):
                dve.wait_ge(x_loaded[t % 2], b * 32 + (t // 2 + 1) * 16)
                tile = xin[:, t % 2, :]
                variance([tile[:, 0:512], tile[:, 512:1024]], t % 2).then_inc(var_ready, 1)
                dve.wait_ge(rstd_ready, b * 3 * TT + t + 1)
                dve.tensor_scalar(tile, tile, mv[:, t % 2, 0:1], rstd[:, t % 2:t % 2 + 1], ALU.subtract,
                                  ALU.mult).then_inc(xn_ready, 1)

            def split_lo(b, ev):
                dve.wait_ge(hi_ready, b * NHI + HI[ev] + 1)
                src, hi, lo = split_views(ev)
                free(dve.tensor_tensor(lo, src, hi, ALU.subtract), ev)

            def maxima(b, ev):
                h = ev[1]
                wait_full(dve, b, ev)
                settle(dve)
                for t in range(TT):
                    n = P * (t + 1)
                    sc = slot(ev)[:, MOFF[t]:MOFF[t] + n]
                    ins = dve.tensor_tensor_reduce(
                        out=sc, in0=sc, in1=mask[:, S - n:S], scale=1.0, scalar=NEG, op0=ALU.add, op1=ALU.max,
                        accum_out=mcol[:, h // 8, t, h % 8:h % 8 + 1])
                free(ins, ev)

            def probabilities_lo(b, h):
                dve.wait_ge(phi_ready, b * NH + h + 1)
                dve.tensor_tensor(p_hl[:, h % 2, 1, :], p32[:, h % 2, :], p_hl[:, h % 2, 0, :],
                                  ALU.subtract).then_inc(plo_ready, 1)

            def normalise(b, h):
                dve.wait_ge(pv_full, b * NH + h + 1)
                o = pv_ps[h % 2].rearrange("p (t d) -> p t d", t=TT)
                wait(dve, pv_free, b * NH + h - 1)
                r = rsum[:, h % 2]
                link(dve.reciprocal(r, o[:, :, HD:HD + 1]))
                dve.tensor_tensor(attn[:, :, HD * h:HD * h + HD], o[:, :, 0:HD], r.broadcast_to([P, TT, HD]),
                                  ALU.mult).then_inc(pv_free, 1)

            def residual(b, ev):
                t = ev[1]
                y = slot(ev)[:, 0:D]
                wait_full(dve, b, ev)
                variance([y[:, 0:512], y[:, 512:1024]], 0, out_f).then_inc(var_ready, 1)
                dve.wait_ge(rstd_ready, b * 3 * TT + TT + 2 * t + 1)
                link(dve.tensor_scalar(rs2[:, 0:1], rstd[:, 0:1], out_f, None, ALU.mult))
                if t >= 2:
                    dve.wait_ge(x1_stored[t % 2], b * 32 + 16)
                r = x1[:, t % 2, :]
                free(dve.tensor_scalar(r, y, mv[:, 0, 0:1], rs2[:, 0:1], ALU.subtract, ALU.mult), ev)
                wait_free(dve, b, ev)
                dve.wait_ge(xr_loaded[t % 2], b * 32 + (t // 2 + 1) * 16)
                dve.tensor_tensor(r, r, xr[:, t % 2, :], ALU.add).then_inc(x1_ready, 1)
                dve.wait_ge(x1_ready, b * TT + t + 1)
                variance([r[:, 0:512], r[:, 512:1024]], 1).then_inc(var_ready, 1)
                dve.wait_ge(rstd_ready, b * 3 * TT + TT + 2 * t + 2)
                if t >= 2:
                    wait_full(dve, b, ("T3", t - 2))
                dve.tensor_scalar(xn2[:, t % 2, :], r, mv[:, 1, 0:1], rstd[:, 1:2], ALU.subtract,
                                  ALU.mult).then_inc(xn_ready, 1)

            def batch(b):
                for ev in events:
                    kind, i = ev
                    if ev == ("T1", 0):
                        layer_norm_in(b, 0)
                        if is_first(b):
                            weight_factor(0)
                        layer_norm_in(b, 1)
                        if is_first(b):
                            weight_factor(1)
                            weight_lo(0)
                            weight_lo(1)
                    if kind in SPLIT:
                        if is_first(b) and ev == ("T1", 2):
                            pass
                        if is_first(b) and ev == ("Q", 0):
                            weight_factor(2)
                            weight_lo(2)
                        split_lo(b, ev)
                        if kind == "T1" and i < 2:
                            layer_norm_in(b, i + 2)
                    elif kind == "M":
                        maxima(b, ev)
                    elif kind == "S":
                        if is_first(b) and i == 0:
                            weight_factor(3)
                            weight_lo(3)
                            scale_tables()
                        if i >= 1:
                            probabilities_lo(b, i - 1)
                    elif kind == "END":
                        probabilities_lo(b, NH - 1)
                    elif kind == "PV":
                        if i >= 1:
                            normalise(b, i - 1)
                        if i == NH - 1:
                            normalise(b, i)
                    elif kind == "MT":
                        dve.wait_ge(mhi_ready, b * NU + i + 1)
                        free(dve.scalar_tensor_tensor(out=mrow[0:8, 1, :], in0=slot(ev)[0:8, 0:S],
                                                      scalar=-1.0 / MAX_UNIT, in1=mrow[0:8, 0, :], op0=ALU.mult,
                                                      op1=ALU.subtract), ev)
                    elif kind == "WO":
                        residual(b, ev)

            dve.wait_ge(consts_ready, 3)
            batch(0)
            per, first_steps = TT * 2 + NH + TT * 6, steps["n"]
            with dve.Fori(1, NB - 1) as b:
                steps["base"], steps["n"] = b * per + (first_steps - per), 0
                batch(b)
                assert steps["n"] == per, steps["n"]
            steps["base"], steps["n"] = (NB - 2) * per + first_steps, 0
            batch(NB - 1)

            def tile(n, par):
                first = isinstance(n, int) and n == 0
                units = unit_list(n)
                if first:
                    dve.tensor_copy(gu_sc[:, 0, :], all_scales[:, 0, :]).then_inc(gusc_ready, 1)
                for u in units:
                    kind, j = u
                    ps = ffn_slot[units[u][0]]
                    done = unit_free[units[u][0]]
                    if kind == "g":
                        w, g, c = gu_parts(j)
                        if j in AT_H and not first:
                            hidden(n - 1, 1 - par, unit_list(n - 1), AT_H.index(j))
                        if j in AT_LO and not first:
                            hidden_lo(n - 1, 1 - par, AT_LO.index(j))
                        if g > 0:
                            unit_filled(dve, units, u)
                            unit_done(dve, units, ("g", j - 2))
                            a = (gacc[:, par] if w == 0 else uacc)[:, c * HALF:c * HALF + HALF]
                            dve.scalar_tensor_tensor(out=a, in0=ps, scalar=gu_sc[:, par, 8 * w + g:8 * w + g + 1],
                                                     in1=a, op0=ALU.mult, op1=ALU.add).then_inc(done, 1)
                        if j == 12 and not (isinstance(n, int) and n == NT - 1):
                            wait(dve, d_conv, n)
                            dve.tensor_copy(gu_sc[:, 1 - par, :], all_scales[:, n + 1, :]).then_inc(gusc_ready, 1)
                    elif j in DVE_D:
                        down_unit(n, par, units, u)
                carried = [u for u in units if u[0] == "c" and u[1] not in DVE_D]
                if carried:
                    unit_done(dve, units, carried[-1])
                dve.tensor_copy(dn_sc[:, par, :], all_scales[:, n, 16:24]).then_inc(dnsc_ready, 1)
            def hidden(m, par, units, c):
                unit_done(dve, units, ("g", GU - 2 + c))
                dve.wait_ge(silu_done, m * 2 + c + 1)
                ua = uacc[:, c * HALF:c * HALF + HALF]
                dve.tensor_tensor(ua, ua, gacc[:, par, c * HALF:c * HALF + HALF], ALU.mult).then_inc(h32_ready, 1)

            def hidden_lo(m, par, c):
                dve.wait_ge(hhi_ready, m * 2 + c + 1)
                dve.tensor_tensor(hid[:, par, 1, c * HALF:c * HALF + HALF], uacc[:, c * HALF:c * HALF + HALF],
                                  hid[:, par, 0, c * HALF:c * HALF + HALF], ALU.subtract).then_inc(h_ready, 1)

            def down_unit(n, par, units, u):
                o, c = u[1] // 2, u[1] % 2
                unit_filled(dve, units, u)
                dve.wait_ge(dnsc_ready, n)
                a = acc[:, o, c * HALF:c * HALF + HALF]
                dve.scalar_tensor_tensor(out=a, in0=ffn_slot[units[u][0]], scalar=dn_sc[:, par if u[0] == "c" else 1 - par, o:o + 1], in1=a,
                                         op0=ALU.mult, op1=ALU.add).then_inc(unit_free[units[u][0]], 1)

            dve.wait_ge(acc_zero, 1)
            over_tiles(dve, tile)
            for c in range(2):
                hidden(NT - 1, 1, unit_list(NT - 1), c)
            for c in range(2):
                hidden_lo(NT - 1, 1, c)
            units = unit_list(NT)
            for u in units:
                if u[1] in DVE_D:
                    down_unit(NT, 0, units, u)

            for f in range(NF + 2):
                if f < NF:
                    i = f % 2
                    y = ffn_slot[f % 4]
                    dve.wait_ge(unit_full[f % 4], F0 + f // 4 + 1)
                    if f >= 2:
                        dve.wait_ge(unit_free[(f - 2) % 4], F0 + (f - 2) // 4 + 1)
                    variance([y[:, 0:512], y[:, 512:1024]], i).then_inc(fvar_ready, 1)
                if 1 <= f <= NF:
                    i = (f - 1) % 2
                    dve.wait_ge(frstd_ready, f)
                    dve.tensor_scalar(rs2[:, i:i + 1], mv[:, i, 0:1], rstd[:, i:i + 1], -1.0, ALU.mult,
                                      ALU.mult).then_inc(fnmr_ready, 1)
                if f >= 2:
                    g = f - 2
                    dve.wait_ge(unit_free[g % 4], F0 + g // 4 + 1)
                    dve.wait_ge(x1b_loaded[g % 4], 16 * (g // 4 + 1))
                    dve.tensor_tensor(y_t[:, g % 4, :], y_t[:, g % 4, :], x1_b[:, g % 4, :],
                                      ALU.add).then_inc(out_ready, 1)

        @block.tensor
        def _(pe):
            def products(dst, terms, n):
                pairs = ((0, 0), (0, 1), (1, 0))
                for k in range(n):
                    for m, (a, c) in enumerate(pairs):
                        lhs, rhs = terms(a, c, k)
                        ins = pe.matmul(dst, lhs, rhs, start=(k == 0 and m == 0), stop=(k == n - 1 and m == 2))
                return ins

            def transposes(dst, src, n, width=P):
                for k in range(n):
                    ins = pe.transpose(dst(k), src(k), ident)
                return ins

            def inputs_of(ev):
                kind, i = ev
                if kind == "K":
                    return [("T1", TT - 2), ("T1", TT - 1)]
                if kind == "MT":
                    return [("M", 8 * i + 6), ("M", 8 * i + 7)]
                return [("T2", i)] if kind == "WO" else []

            def enter(b, ev):
                need = {J[ev] % 2: J[ev] // 2}
                for job in inputs_of(ev):
                    need[J[job] % 2] = max(need.get(J[job] % 2, 0), J[job] // 2 + 1)
                for parity, count in need.items():
                    wait(pe, slot_free[parity], b * (NJ // 2) + count)

            def batch(b):
                for ev in events:
                    kind, i = ev
                    if ev in J:
                        enter(b, ev)
                    if kind == "T1":
                        pe.wait_ge(xn_ready, b * 2 * TT + i + 1)
                        full(transposes(lambda k: slot(ev)[:, P * k:P * k + P],
                                        lambda k: xin[:, i % 2, P * k:P * k + P], KD), ev)
                    elif kind == "K":
                        if is_first(b) and i == 0:
                            pe.wait_ge(wlo_ready, 2)
                        full(products(slot(ev)[:, 0:S], lambda a, c, k: (w_k[:, a, k, P * i:P * i + P], xnt[:, c, k, :]),
                                      KD), ev)
                    elif kind == "V":
                        for t in range(2):
                            tok = P * (2 * i + t)
                            ins = products(slot(ev)[:, 256 * t:256 * t + 256],
                                           lambda a, c, k: (xnt[:, a, k, tok:tok + P], w_v[:, c, k, :]), KD)
                        full(ins, ev)
                    elif kind == "Q":
                        if is_first(b) and i == 0:
                            pe.wait_ge(wlo_ready, 3)
                        full(products(slot(ev)[:, 0:S], lambda a, c, k: (w_q[:, a, k, P * i:P * i + P], xnt[:, c, k, :]),
                                      KD), ev)
                    elif kind == "M":
                        if i % 8 == 0:
                            u = i // 8
                            pe.wait_ge(ks_stacked, (b + 1) * 192)
                            pe.wait_ge(qs_stacked[u % 2], b * 384 + (u // 2 + 1) * 192)
                        for t in (3, 2, 0, 1):
                            n = P * (t + 1)
                            ins = pe.matmul(slot(ev)[:, MOFF[t]:MOFF[t] + n], q_s[0:3 * HD, i, P * t:P * t + P],
                                            k_s[0:3 * HD, i // NREP, 0:n], start=True, stop=True)
                        full(ins, ev)
                    elif kind == "MT":
                        full(transposes(lambda t: slot(ev)[0:8, P * t:P * t + P], lambda t: mcol[:, i, t, :], TT), ev)
                    elif kind == "S":
                        if i % 8 == 0:
                            pe.wait_ge(mrow_loaded, (b * NU + i // 8 + 1) * 32)
                        for j in range(TT):
                            ins = pe.matmul(slot(ev)[:, KOFF[j]:KOFF[j] + KLEN[j]],
                                            k_s[0:SOFTMAX_ROWS, i // NREP, P * j:P * j + P],
                                            q_s[0:SOFTMAX_ROWS, i, P * j:S], start=True, stop=True)
                        full(ins, ev)
                    elif kind == "PV":
                        pe.wait_ge(plo_ready, b * NH + i + 1)
                        wait(pe, pv_free, b * NH + i - 1)
                        g = i // NREP
                        for t in range(TT):
                            dst = pv_ps[i % 2][:, 33 * t:33 * t + 33]
                            for j in range(t + 1):
                                cols = slice(KOFF[j] + P * (t - j), KOFF[j] + P * (t - j) + P)
                                hi, lo = p_hl[:, i % 2, 0, cols], p_hl[:, i % 2, 1, cols]
                                pe.matmul(dst, hi, v_a[:, j, g, :], start=(j == 0), stop=False)
                                pe.matmul(dst, hi, v_b[:, j, g, :], start=False, stop=False)
                                ins = pe.matmul(dst, lo, v_a[:, j, g, :], start=False, stop=(j == t))
                        ins.then_inc(pv_full, 1)
                    elif kind == "T2":
                        pe.wait_ge(pv_free, (b + 1) * NH)
                        full(transposes(lambda k: slot(ev)[:, P * k:P * k + P],
                                        lambda k: attn[:, i, P * k:P * k + P], KD), ev)
                    elif kind == "WO":
                        for m in range(2):
                            ins = products(slot(ev)[:, 512 * m:512 * m + 512],
                                           lambda a, c, k: (at_t[:, a, k, P * i:P * i + P],
                                                            w_o[:, c, k, 512 * m:512 * m + 512]), KD)
                        full(ins, ev)
                    elif kind == "T3":
                        pe.wait_ge(xn_ready, b * 2 * TT + TT + i + 1)
                        full(transposes(lambda k: slot(ev)[:, P * k:P * k + P],
                                        lambda k: xn2[:, i % 2, P * k:P * k + P], KD), ev)

            pe.wait_ge(ident_ready, 2)
            over_batches(pe, batch)
            wait_free(pe, NB - 1, ("T3", TT - 2))
            wait_free(pe, NB - 1, ("T3", TT - 1))

            def gu_unit(n, par, units, u):
                w, g, c = gu_parts(u[1])
                s, _ = units[u]
                for m in range(2):
                    b = 2 * c + m
                    for hl in range(2):
                        ins = pe.matmul(ffn_slot[s][:, S * m:S * m + S], w_gu[:, par, w, g, :], xt[:, b, hl, g, :],
                                        start=(hl == 0), stop=(hl == 1))
                ins.then_inc(unit_full[s], 1)

            def down_unit(n, par, units, u):
                o, c = u[1] // 2, u[1] % 2
                dpar = par if u[0] == "c" else 1 - par
                s, _ = units[u]
                for m in range(2):
                    at = c * HALF + S * m
                    for hl in range(2):
                        ins = pe.matmul(ffn_slot[s][:, S * m:S * m + S], w_d[:, dpar, P * o:P * o + P],
                                        hid[:, dpar, hl, at:at + S], start=(hl == 0), stop=(hl == 1))
                ins.then_inc(unit_full[s], 1)

            def tile(n, par):
                units = unit_list(n)
                first_d = True
                for u in units:
                    s, before = units[u]
                    wait(pe, unit_free[s], before)
                    if u[0] == "g":
                        if u[1] == 0:
                            pe.wait_ge(gu_conv, n + 1)
                        if isinstance(n, int) and n == 0 and u[1] < 2:
                            pe.wait_ge(xt_loaded[2 * u[1]], 16)
                            pe.wait_ge(xt_loaded[2 * u[1] + 1], 16)
                        gu_unit(n, par, units, u)
                    else:
                        if u[0] == "d" and first_d:
                            pe.wait_ge(d_conv, n)
                            pe.wait_ge(h_ready, n * 2)
                            first_d = False
                        down_unit(n, par, units, u)

            over_tiles(pe, tile)
            tile(NT, NT % 2)
            lasts = unit_list(NT)
            half_pool = [[number for u, number, _ in pool_units(NT) if u[0] == "c" or u[1] % 2 <= c][-1] for c in range(2)]
            half_dve = [[u for u in lasts if u[0] == "d" and u[1] % 2 == c and u[1] in DVE_D][-1:] for c in range(2)]
            for f in range(NF):
                c = f // (NF // 2)
                if f % (NF // 2) == 0:
                    pe.wait_ge(tmp_free, RT + half_pool[c] + 1)
                    for u in half_dve[c]:
                        unit_done(pe, lasts, u)
                pe.wait_ge(unit_free[f % 4], F0 + f // 4)
                for k in range(KD):
                    ins = pe.transpose(ffn_slot[f % 4][:, P * k:P * k + P], acc[:, k, f * P:f * P + P], ident)
                ins.then_inc(unit_full[f % 4], 1)


_SHAPES = [((4, 512, 1024), "float32")]


def kernel(L0_attn_x, L0_attn_wq, L0_attn_wk, L0_attn_wv, L0_attn_wo, L0_ffn_gate_q, L0_ffn_gate_s,
           L0_ffn_up_q, L0_ffn_up_s, L0_ffn_down_q, L0_ffn_down_s):
    import numpy as np
    import concourse.bacc as bacc
    from concourse import mybir as mb
    from concourse.bass_utils import run_bass_kernel_spmd

    p = 128
    x = np.asarray(L0_attn_x)
    gate, up, down = (np.asarray(a) for a in (L0_ffn_gate_q, L0_ffn_up_q, L0_ffn_down_q))
    gate_s, up_s, down_s = (np.asarray(a) for a in (L0_ffn_gate_s, L0_ffn_up_s, L0_ffn_down_s))
    inter, width = gate.shape
    nt, kd = inter // p, width // p
    gu = np.stack([gate, up]).reshape(2, nt, p, kd, p).transpose(1, 4, 0, 3, 2).reshape(nt, p, 2 * kd * p)
    dn = down.reshape(width, nt, p).transpose(1, 2, 0)
    sc = np.concatenate([gate_s.reshape(nt, p, kd), up_s.reshape(nt, p, kd),
                         down_s.reshape(kd, p, nt).transpose(2, 1, 0)], axis=2)
    arrays = {"x": x, "wq": L0_attn_wq, "wk": L0_attn_wk, "wv": L0_attn_wv, "wo": L0_attn_wo,
              "gu_t": gu, "down_t": dn, "scales": sc}
    arrays = {k: np.ascontiguousarray(v) for k, v in arrays.items()}

    nc = bacc.Bacc("TRN2", target_bir_lowering=False, num_devices=1)
    aps = {k: nc.dram_tensor(f"in_{k}", v.shape, mb.dt.from_np(v.dtype), kind="ExternalInput").ap()
           for k, v in arrays.items()}
    out = nc.dram_tensor("out_0", (x.shape[0] * x.shape[1], x.shape[2]), mb.dt.float32, kind="ExternalOutput").ap()
    sandwich(nc, out=out, **aps)
    r = run_bass_kernel_spmd(nc, [{f"in_{k}": v for k, v in arrays.items()}], core_ids=[0])
    return r.results[0]["out_0"].reshape(x.shape)
```

```python
from contextlib import ExitStack

import concourse.bass as bass
from concourse import mybir

F32 = mybir.dt.float32
F16 = mybir.dt.float16
BF16 = mybir.dt.bfloat16
I32 = mybir.dt.int32
ALU = mybir.AluOpType
ACT = mybir.ActivationFunctionType
AX = mybir.AxisListType

P = 128
HD = 32
SOFTMAX_ROWS = 98
MAX_UNIT = 32768.0


def sandwich(nc, x, wq, wk, wv, wo, gu_t, down_t, scales, out):
    NB, S, D = x.shape
    NH = wq.shape[1] // HD
    NKV = wk.shape[1] // HD
    NREP = NH // NKV
    KD = D // P
    TT = S // P
    NT = gu_t.shape[0]
    NTOK = NB * S
    HALF = 2 * S
    NU = NH // 8
    EPS = 1e-5
    assert HD * NREP == P and KD == 8 and TT == 4 and S == 512 and NB == 4 and NKV == 8

    x1_scr = nc.dram_tensor("x1_scratch", [NB, TT, P, D], F32, kind="Internal").ap()
    xt_scr = nc.dram_tensor("xt_scratch", [NB, TT, P, 2 * KD * P], F16, kind="Internal").ap()

    NEG = -1.0e30
    EARLY = NKV - 2
    GROUPS = [(t, g) for t in (0, 1) for g in range(EARLY)] + [(t, g) for t in (0, 1) for g in range(EARLY, NKV)]
    GROUPS += [(t, g) for t in range(2, TT) for g in range(NKV)]
    GROUP_NO = {tg: n for n, tg in enumerate(GROUPS)}
    NG2 = len(GROUPS) // 2
    banks = [(t, g, j) for t, g in GROUPS for j in range(t + 1)]
    S_UNITS = [banks[i:i + 2] for i in range(0, len(banks), 2)]
    NS = len(S_UNITS)
    MASKED = [any(j == t for t, _, j in u) for u in S_UNITS]
    NM = sum(MASKED)
    assert all(GROUPS[n + 1] == (GROUPS[n][0], GROUPS[n][1] + 1) for n in range(0, len(GROUPS), 2))
    LATE_UNIT = [any(g >= EARLY for _, g, _ in u) for u in S_UNITS].index(True)
    PB = 4
    LAG = 3

    with ExitStack() as ctx:
        ARENA = 53200
        arena = ctx.enter_context(nc.sbuf_tensor("arena", [P, ARENA], F32))
        place = {"at": 0}

        def carve(words, dtype=F32, at=None):
            if at is None:
                at = place["at"]
                place["at"] = at + words
                assert place["at"] <= ARENA, place["at"]
            v = arena[:, at:at + words]
            return v if dtype == F32 else v.bitcast(dtype)

        ident = carve(P)
        all_scales = carve(NT * 25).rearrange("p (n c) -> p n c", n=NT)
        gu_sc = carve(2 * 25).rearrange("p (b c) -> p b c", b=2)
        dn_sc = carve(2 * 8).rearrange("p (b c) -> p b c", b=2)
        neg_half = carve(1)
        score_f = carve(1)
        out_f = carve(1)
        stats = carve(4 * 12).rearrange("p (b c) -> p b c", b=4)
        mv = carve(4 * 2).rearrange("p (b c) -> p b c", b=4)
        vpe = carve(4)
        rstd = carve(4)
        rs2 = carve(2)
        base = place["at"]

        w_q = carve(8192, F16).rearrange("p (s k n) -> p s k n", s=2, k=KD)
        w_k = carve(2048, F16).rearrange("p (s k n) -> p s k n", s=2, k=KD)
        w_v = carve(2048, F16).rearrange("p (s k n) -> p s k n", s=2, k=KD)
        w_o = carve(8192, F16).rearrange("p (s k n) -> p s k n", s=2, k=KD)
        XB = 3
        X_LOADS = [2, 1, 1]
        xin = carve(XB * D).rearrange("p (b n) -> p b n", b=XB)
        xnt = carve(4096, F16).rearrange("p (s k n) -> p s k n", s=2, k=KD)
        p32 = carve(PB * 1024, at=place["at"] - 4096).rearrange("p (b n) -> p b n", b=PB)
        qt_at = place["at"]
        qt = carve(2048, F16).rearrange("p (s b m n) -> p s b m n", s=2, b=2, m=2)
        qs_at = place["at"]
        q_s = carve(8192, F16).rearrange("p (h n) -> p h n", h=NH)
        k_s = carve(2048, F16).rearrange("p (g n) -> p g n", g=NKV)
        v_a = carve(TT * NKV * 33 // 2, F16).rearrange("p (t g d) -> p t g d", t=TT, g=NKV)
        v_b = carve(TT * NKV * 33 // 2, F16).rearrange("p (t g d) -> p t g d", t=TT, g=NKV)
        p_at = place["at"]
        xb = carve(D)
        p_hl = carve(PB * 1024, F16).rearrange("p (b s n) -> p b s n", b=PB, s=2)
        attn = carve(2 * D).rearrange("p (b n) -> p b n", b=2)
        x2t = carve(KD * P, F16).rearrange("p (s k n) -> p s k n", s=2, k=KD)
        at_t = carve(2 * KD * P, F16, at=qt_at).rearrange("p (b s k n) -> p b s k n", b=2, s=2, k=KD)
        xr_at = place["at"]
        xr = carve(2 * D).rearrange("p (b n) -> p b n", b=2)
        mask = carve(S // 2, BF16)
        mcol = carve(NH * TT).rearrange("p (t h) -> p t h", t=TT)
        mrow = carve(S, F16).rearrange("p (s n) -> p s n", s=2)
        wabs = carve(4)
        wall = carve(4)
        wpow = carve(4)
        wfac = carve(4)
        rsum = carve(2 * 2 * NREP).rearrange("p (b t d) -> p b t d", b=2, d=1)
        stage_q = carve(8192, at=qs_at).rearrange("p (k n) -> p k n", k=KD)
        stage_o = carve(8192, at=p_at).rearrange("p (k n) -> p k n", k=KD)
        stage_k = carve(2048, at=xr_at).rearrange("p (k n) -> p k n", k=KD)
        stage_v = carve(2048, at=qt_at).rearrange("p (k n) -> p k n", k=KD)
        place["at"] = base
        xt = carve(NB * 4096, F16).rearrange("p (t s k n) -> p t s k n", t=NB * TT, s=2, k=KD)
        xt_flat = carve(NB * 4096, F16, at=base).rearrange("p (t n) -> p t n", t=NB * TT)
        acc = carve(KD * NTOK).rearrange("p (o n) -> p o n", o=KD)
        gacc = carve(2 * NTOK).rearrange("p (b n) -> p b n", b=2)
        uacc = carve(NTOK)
        hid = carve(2 * NTOK, F16).rearrange("p (b s n) -> p b s n", b=2, s=2)
        RT = 3
        tmp = carve(RT * HALF).rearrange("p (r n) -> p r n", r=RT)
        int_gu = carve(2 * KD * P, I32)
        int_d = carve(D, I32)
        w_gu = carve(2 * KD * P, BF16).rearrange("p (b w k n) -> p b w k n", b=2, w=2, k=KD)
        w_d = carve(D, BF16).rearrange("p (b n) -> p b n", b=2)
        y_t = carve(4 * D, at=base).rearrange("p (b n) -> p b n", b=4)
        x1_b = carve(4 * D, at=base + 4 * D).rearrange("p (b n) -> p b n", b=4)

        psum = ctx.enter_context(nc.psum_tensor("psum", [P, 8 * 512], F32))
        job_slot = [psum[:, 0:1024], psum[:, 1024:2048]]
        wide_ps = psum[:, 2048:3072]
        pv_ps = [psum[:, 3072:3336], psum[:, 3584:3848]]
        ffn_slot = [psum[:, 1024 * s:1024 * s + 1024] for s in range(4)]

        def sem(name):
            return ctx.enter_context(nc.semaphore(name))

        ident_ready = sem("ident_ready")
        consts_ready = sem("consts_ready")
        settled = sem("settled")
        x_loaded = [sem(f"x_loaded{i}") for i in range(XB)]
        w_loaded = [sem(f"w_loaded{i}") for i in range(4)]
        s_loaded = sem("s_loaded")
        wabs_ready = sem("wabs_ready")
        wall_ready = sem("wall_ready")
        wfac_ready = sem("wfac_ready")
        whi_ready = sem("whi_ready")
        wlo_ready = sem("wlo_ready")
        dve_step = sem("dve_step")
        scales_ready = sem("scales_ready")
        var_ready = [sem(f"var_ready{i}") for i in range(2)]
        rstd_ready = [sem(f"rstd_ready{i}") for i in range(2)]
        xn_ready = [sem(f"xn_ready{i}") for i in range(2)]
        slot_full = [sem(f"slot_full{i}") for i in range(2)]
        slot_free = [sem(f"slot_free{i}") for i in range(2)]
        hi_ready = sem("hi_ready")
        ks_stacked = sem("ks_stacked")
        qs_stacked = [sem(f"qs_stacked{i}") for i in range(2)]
        wide_full = sem("wide_full")
        wide_free = sem("wide_free")
        mrow_loaded = sem("mrow_loaded")
        p_masked = sem("p_masked")
        phi_ready = sem("phi_ready")
        plo_ready = sem("plo_ready")
        pv_done = sem("pv_done")
        pv_free = sem("pv_free")
        xr_loaded = [sem(f"xr_loaded{i}") for i in range(2)]
        x1_ready = sem("x1_ready")
        x1_stored = [sem(f"x1_stored{i}") for i in range(2)]
        x2t_stored = sem("x2t_stored")
        xt_loaded = [sem(f"xt_loaded{b}") for b in range(NB)]
        acc_zero = sem("acc_zero")
        unit_full = [sem(f"unit_full{s}") for s in range(4)]
        unit_free = [sem(f"unit_free{s}") for s in range(4)]
        gu_loaded = sem("gu_loaded")
        d_loaded = sem("d_loaded")
        gu_conv = sem("gu_conv")
        d_conv = sem("d_conv")
        gusc_ready = sem("gusc_ready")
        dnsc_ready = sem("dnsc_ready")
        silu_done = sem("silu_done")
        h32_ready = sem("h32_ready")
        hhi_ready = sem("hhi_ready")
        h_ready = sem("h_ready")
        tmp_free = sem("tmp_free")
        fvar_ready = sem("fvar_ready")
        frstd_ready = sem("frstd_ready")
        fnmr_ready = sem("fnmr_ready")
        x1b_loaded = [sem(f"x1b_loaded{i}") for i in range(4)]
        out_ready = sem("out_ready")
        out_stored = [sem(f"out_stored{i}") for i in range(4)]

        def settle(eng):
            eng.sem_inc(settled, 1)

        def wait(eng, s, value):
            if not isinstance(value, int):
                eng.wait_ge(s, value)
                if eng is nc.sync:
                    settle(eng)
            elif value > 0:
                eng.wait_ge(s, value)

        def max_jobs(m):
            return [("MA", 4 * m), ("MA", 4 * m + 1), ("MB", 2 * m), ("MA", 4 * m + 2), ("MA", 4 * m + 3), ("MB", 2 * m + 1)]

        LATE_STEPS = [("R", 4 * (TT - 1) + 2), ("R", 4 * (TT - 1) + 3), ("T3", TT - 1)]
        events = []
        maxima_left = [(8 * (m // 2) + 21, job) for m in range(8) for job in max_jobs(m)]
        proj = [("K", 0), ("K", 1)] + [("Q", m) for m in range(8)] + [("V", 0), ("V", 1)]
        for n in range(4 * len(proj)):
            events += [("PP", (proj[n // 4], n % 4))]
            if n % 4 == 3:
                events += [proj[n // 4]]
            if n in (4, 6, 8):
                events += [LATE_STEPS[(n - 4) // 2]]
            for _ in range(1 + n % 2):
                if maxima_left and maxima_left[0][0] <= n:
                    events += [maxima_left.pop(0)[1]]
        late = [job for _, job in maxima_left if job[1] >= (24 if job[0] == "MA" else 12)]
        events += [job for _, job in maxima_left if job not in late] + [("MT", 0)]
        behind = {14: [("T2", 0)], 17: [("T2", 1)], 29: [("T2", 2)],
                  31: [("LN", 0)], 32: [("LX", 0)], 33: [("LN", 1)], 34: [("LX", 1)], 36: [("LN", 2)], 37: [("LX", 2)]}
        for t, u in ((0, 15), (1, 23), (2, 31)):
            for i in range(8):
                behind.setdefault(u + i, []).append(("WP", 8 * t + i))
            behind[u + 7].append(("WO", t))
            for i in range(4):
                if u + 7 + i < NS:
                    behind.setdefault(u + 7 + i, []).append(("R", 4 * t + i))
            if u + 12 < NS:
                behind.setdefault(u + 12, []).append(("T3", t))
        for n in range(0, len(late), 2):
            behind.setdefault(n // 2, [])[0:0] = late[n:n + 2]
        assert len(late) // 2 < LATE_UNIT
        behind.setdefault((len(late) + 1) // 2, []).append(("MT", 1))
        for u in range(NS):
            events += [("S", u)] + ([("PV", u - LAG)] if u >= LAG else []) + behind.get(u, [])
        events += [("END", 0)] + [("PV", NS - LAG + i) for i in range(LAG)]
        events += [("END", 1), ("R", 10), ("T1", 0), ("LN", 3), ("T1", 1), ("R", 11), ("T2", 3), ("LX", 3)]
        events += [("WP", 24 + i) for i in range(3)] + [("T1", 2)] + [("WP", 27 + i) for i in range(2)] + [("T3", 2)]
        events += [("WP", 29 + i) for i in range(3)] + [("WO", 3), ("R", 12), ("T1", 3), ("R", 13)]
        epilogue = LATE_STEPS
        prologue = [("LN", 0), ("LN", 1), ("T1", 0), ("LN", 2), ("T1", 1), ("LN", 3), ("T1", 2), ("T1", 3)]
        SLOT_KINDS = ("T1", "MA", "MB", "S", "T2", "T3")
        SPLIT = ("T1", "K", "V", "Q", "T2", "T3")
        WIDE = {job: n for n, job in enumerate([e for e in events if e[0] in ("K", "Q", "V", "MT", "WO")])}
        NW = len(WIDE)

        def wide_bank(job):
            return wide_ps[:, 512 * (WIDE[job] % 2):512 * (WIDE[job] % 2) + 512]

        def wide_wait(eng, b, job):
            n = WIDE[job]
            wait(eng, wide_free, b * NW + (n if job[0] == "WO" or n < 1 else n - 1))

        def head_range(i):
            return (0, NREP * EARLY) if i == 0 else (NREP * EARLY, NH)

        def is_first(b):
            return isinstance(b, int) and b == 0

        def is_last(b):
            return isinstance(b, int) and b == NB - 1

        def events_of(b):
            return [e for e in events if not (is_last(b) and e[0] in ("T1", "LN", "LX"))
                    and not (is_first(b) and e in LATE_STEPS)]

        def owner(b, ev):
            return b + 1 if ev[0] in ("T1", "LN", "LX") else b - 1 if ev in LATE_STEPS else b

        class Numbers:

            def __init__(self, kinds):
                lists = [[e for e in events_of(b) if e[0] in kinds] for b in (0, None, NB - 1)]
                self.first, self.middle, self.last = [{e: n for n, e in enumerate(es)} for es in lists]
                self.start = TT + len(self.first)
                self.per = len(self.middle)

            def of(self, b, job):
                if job[0] == "T1":
                    return (0, job[1]) if is_first(b) else self.in_list(b - 1, job)
                if job in LATE_STEPS:
                    return self.in_list(b + 1, job)
                return self.in_list(b, job)

            def in_list(self, b, job):
                if isinstance(b, int) and b == 0:
                    return 0, TT + self.first[job]
                if isinstance(b, int) and b == NB:
                    return NB - 2, self.start + len(self.last) + [e for e in epilogue if e[0] == "T3"].index(job)
                table = self.last if is_last(b) else self.middle
                return b - 1, self.start + table[job]

        SLOTS, HIS = Numbers(SLOT_KINDS), Numbers(SPLIT + ("MT",))
        assert SLOTS.per % 2 == 0

        def slot_number(b, job):
            before, n = SLOTS.of(b, job)
            return n % 2, before * (SLOTS.per // 2) + n // 2

        def slot(b, job):
            return job_slot[slot_number(b, job)[0]]

        def wait_full(eng, b, job):
            s, n = slot_number(b, job)
            wait(eng, slot_full[s], n + 1)

        def wait_free(eng, b, job):
            s, n = slot_number(b, job)
            wait(eng, slot_free[s], n + 1)

        def full(ins, b, job):
            ins.then_inc(slot_full[slot_number(b, job)[0]], 1)

        def free(ins, b, job):
            ins.then_inc(slot_free[slot_number(b, job)[0]], 1)

        def split_views(b, job):
            kind, i = job
            if kind == "V":
                src = wide_bank(job).rearrange("p (t g d) -> p t g d", t=2, g=NKV)
                return src, v_a[:, 2 * i:2 * i + 2, :, 0:HD], v_b[:, 2 * i:2 * i + 2, :, 0:HD]
            if kind == "K":
                return wide_bank(job), qt[:, 0, 1, i, :], qt[:, 1, 1, i, :]
            if kind == "Q":
                u = i // 2
                return wide_bank(job), qt[:, 0, u % 2, i % 2, :], qt[:, 1, u % 2, i % 2, :]
            ps = slot(b, job)
            src = ps.rearrange("p (k n) -> p k n", k=KD)
            if kind == "T1":
                return src, xnt[:, 0, :, P * i:P * i + P], xnt[:, 1, :, P * i:P * i + P]
            dst = at_t[:, i % 2] if kind == "T2" else x2t
            return src, dst[:, 0], dst[:, 1]

        def max_parts(job):
            kind, i = job
            if kind == "MA":
                return [(i, 3, 0), (i, 2, 512), (i, 0, 896)]
            return [(2 * i, 1, 0), (2 * i + 1, 1, 256)]

        GU = 4 * KD
        DN = 2 * KD
        AT_H, AT_HI, AT_LO = [1, 2], [3, 4], [5, 7]
        CARRY = 4
        order_zero = [("g", j) for j in range(GU)]
        order, n_d = [], 0
        for j in range(GU):
            order.append(("g", j))
            if j % 2 and j < 2 * CARRY:
                order.append(("c", DN - CARRY + j // 2))
            while n_d < (DN - CARRY) * (j - 2 * CARRY - 1) // (GU - 2 * CARRY - 2):
                order.append(("d", n_d))
                n_d += 1
        assert n_d == DN - CARRY
        order_one = [u for u in order if u[0] != "c"]
        order_last = [("c", j) for j in range(DN - CARRY, DN)] + [("d", 2 * (j % KD) + j // KD) for j in range(DN)]
        DVE_D = [9]
        NPD = DN - len(DVE_D)
        NPC = len([j for j in range(DN - CARRY, DN) if j not in DVE_D])
        assert NPD % RT == 0 and (GU + DN) % 4 == 0 and GU % 4 == 0 and CARRY % 4 == 0

        def unit_list(n):
            if isinstance(n, int) and n < 2:
                units, before = (order_zero, 0) if n == 0 else (order_one, GU // 4)
            else:
                units = order_last if isinstance(n, int) and n == NT else order
                before = n * ((GU + DN) // 4) - (DN + CARRY) // 4
            return {u: (pos % 4, before + pos // 4) for pos, u in enumerate(units)}

        def pool_units(n):
            us = [u for u in unit_list(n) if u[0] != "g" and u[1] not in DVE_D]
            at = 0 if isinstance(n, int) and n == 1 else (n - 1) * NPD - NPC
            return [(u, at + q, (q - (0 if isinstance(n, int) and n == 1 else NPC)) % RT) for q, u in enumerate(us)]

        def gu_parts(j):
            return j // 16, (j % 16) // 2, j % 2

        def unit_done(eng, units, u):
            s, c = units[u]
            eng.wait_ge(unit_free[s], c + 1)

        def unit_filled(eng, units, u):
            s, c = units[u]
            wait(eng, unit_full[s], c + 1)

        def over_tiles(eng, one_tile):
            one_tile(0, 0)
            one_tile(1, 1)
            with eng.Fori(0, (NT - 4) // 2) as i:
                one_tile(i * 2 + 2, 0)
                one_tile(i * 2 + 3, 1)
            one_tile(NT - 2, 0)
            one_tile(NT - 1, 1)

        def over_batches(eng, one_batch):
            one_batch(0)
            with eng.Fori(1, NB - 1) as b:
                one_batch(b)
            one_batch(NB - 1)

        NF = NTOK // P
        F0 = NT * (GU + DN) // 4

        block = ctx.enter_context(nc.Block())

        @block.sync
        def _(sp):
            x_tiles = x.rearrange("b (t p) n -> b t p n", p=P)

            def load_x(b, t):
                sp.dma_start(xin[:, t % XB, :], x_tiles[b, t]).then_inc(x_loaded[t % XB], 16)

            sp.dma_start(xin[:, 0, :], x_tiles[0, 0]).then_inc(x_loaded[0], 16)
            sp.dma_start(xin[:, 1, :], x_tiles[0, 1]).then_inc(x_loaded[1], 16)
            for n, (dst, src) in enumerate(((stage_k, wk), (stage_v, wv), (stage_q, wq), (stage_o, wo))):
                sp.dma_start(dst, src.rearrange("(k p) n -> p k n", p=P)).then_inc(w_loaded[n], 16)
                if n == 1:
                    load_x(0, 2)
                    wait_full(sp, 0, ("T1", 0))
                    load_x(0, 3)
            sp.dma_start(all_scales[:, :, 0:24], scales.rearrange("n p c -> p n c")).then_inc(s_loaded, 16)

            def stack_queries(b, u):
                if u == 0:
                    if is_first(b):
                        wait(sp, wlo_ready, 3)
                wait(sp, wide_free, b * NW + WIDE[("Q", 2 * u + 1)] + 1)
                for c in range(3):
                    rows = q_s[HD * c:HD * c + HD, 8 * u:8 * u + 8, :].rearrange("p (m r) n -> p m r n", r=NREP)
                    for r in range(NREP):
                        sp.dma_start(rows[:, :, r, :], qt[HD * r:HD * r + HD, 1 if c == 1 else 0, u % 2, :, :])\
                            .then_inc(qs_stacked[u % 2], 16)

            def load_residual(b, t):
                if is_first(b) and t < 2:
                    sp.wait_ge(wlo_ready, 4)
                elif t < 2:
                    wait(sp, x1_stored[t], b * 32)
                else:
                    wait(sp, x1_stored[t % 2], b * 32 + 16)
                    wait(sp, xn_ready[1], b * TT + t - 1)
                sp.dma_start(xr[:, t % 2, :], x_tiles[b, t]).then_inc(xr_loaded[t % 2], 16)

            def store_x1(b, t):
                wait(sp, x1_ready, b * TT + t + 1)
                sp.dma_start(x1_scr[b, t], xr[:, t % 2, :]).then_inc(x1_stored[t % 2], 16)

            def store_x2t(b, t):
                wait_free(sp, b, ("T3", t))
                sp.dma_start(xt_scr[b, t], x2t.rearrange("p s k n -> p (s k n)")).then_inc(x2t_stored, 16)

            def batch(b):
                if not is_last(b):
                    wait_full(sp, b, ("T1", 3))
                    for t in range(XB):
                        load_x(b + 1, t)
                if not is_first(b):
                    store_x1(b - 1, TT - 1)
                wait(sp, wide_free, b * NW + WIDE[("K", 1)] + 1)
                for c in range(3):
                    rows = k_s[HD * c:HD * c + HD, :, :].rearrange("p (m r) n -> p m r n", r=NREP)
                    for r in range(NREP):
                        sp.dma_start(rows[:, :, r, :], qt[HD * r:HD * r + HD, 1 if c == 2 else 0, 1, :, :])\
                            .then_inc(ks_stacked, 16)
                for u in range(NU):
                    stack_queries(b, u)
                    if u == 0 and not is_first(b):
                        store_x2t(b - 1, TT - 1)
                        load_residual(b, 1)
                for m in range(2):
                    first, end = head_range(m)
                    wait(sp, wide_free, b * NW + WIDE[("MT", m)] + 1)
                    for i in range(2):
                        sp.dma_start(q_s[3 * HD + i:3 * HD + i + 1, first:end, :], mrow[0:end - first, i, :])\
                            .then_inc(mrow_loaded, 16)
                load_residual(b, 0)
                if is_first(b):
                    load_residual(b, 1)
                if is_last(b):
                    sp.wait_ge(wide_full, b * NW + WIDE[("V", 1)] + 1)
                    sp.wait_ge(x2t_stored, 16 * TT * b)
                    for i in range(b):
                        sp.dma_start(xt_flat[:, TT * i:TT * i + TT, :], xt_scr[i].rearrange("t p n -> p t n"))\
                            .then_inc(xt_loaded[i], 16)
                for t in range(TT - 1):
                    store_x1(b, t)
                    if t < 2:
                        load_residual(b, t + 2)
                    elif not is_last(b):
                        wait_full(sp, b + 1, ("T1", 0))
                        load_x(b + 1, 3)
                    store_x2t(b, t)

            over_batches(sp, batch)
            wait_full(sp, NB - 1, ("T2", 3))
            sp.dma_start(int_gu, gu_t[0]).then_inc(gu_loaded, 16)
            store_x1(NB - 1, TT - 1)
            store_x2t(NB - 1, TT - 1)
            sp.wait_ge(x2t_stored, 16 * NB * TT)
            sp.dma_start(xt_flat[:, TT * (NB - 1):TT * NB, :], xt_scr[NB - 1].rearrange("t p n -> p t n"))\
                .then_inc(xt_loaded[NB - 1], 16)
            sp.dma_start(int_d, down_t[0]).then_inc(d_loaded, 16)

            def tile(n, par):
                if isinstance(n, int) and n == NT - 1:
                    return
                wait(sp, gu_conv, n + 1)
                sp.dma_start(int_gu, gu_t[n + 1]).then_inc(gu_loaded, 16)
                wait(sp, d_conv, n + 1)
                sp.dma_start(int_d, down_t[n + 1]).then_inc(d_loaded, 16)

            over_tiles(sp, tile)

            last = unit_list(NT - 1)
            for u in order[-4:]:
                unit_filled(sp, last, u)
            for f in range(NF + 2):
                if f < NF:
                    if f >= 4:
                        wait(sp, out_ready, f - 3)
                    sp.dma_start(x1_b[:, f % 4, :], x1_scr[f // TT, f % TT]).then_inc(x1b_loaded[f % 4], 16)
                if f >= 2:
                    g = f - 2
                    wait(sp, out_ready, g + 1)
                    sp.dma_start(out[g * P:g * P + P, :], y_t[:, g % 4, :]).then_inc(out_stored[g % 4], 16)
            for i in range(4):
                wait(sp, out_stored[i], 16 * NF // 4)

        @block.gpsimd
        def _(pool):
            pool.memset(ident, 0.0).then_inc(ident_ready, 1)
            pool.wait_ge(ident_ready, 1)
            pool.affine_select(out=ident, in_=ident, compare_op=ALU.not_equal, fill=1.0, base=0,
                               pattern=[[-1, P]], channel_multiplier=1).then_inc(ident_ready, 1)
            pool.memset(neg_half, -0.5).then_inc(consts_ready, 1)
            pool.memset(mask, 0.0).then_inc(consts_ready, 1)
            pool.wait_ge(consts_ready, 2)
            tri = mask[:, S - P:S]
            pool.affine_select(out=tri, in_=tri, compare_op=ALU.is_ge, fill=NEG, base=0,
                               pattern=[[-1, P]], channel_multiplier=1).then_inc(consts_ready, 1)
            pool.memset(v_a.rearrange("p t g d -> p (t g d)"), 1.0).then_inc(consts_ready, 1)
            pool.memset(v_b.rearrange("p t g d -> p (t g d)"), 0.0).then_inc(consts_ready, 1)
            pool.wait_ge(consts_ready, 5)
            pool.memset(k_s[3 * HD:SOFTMAX_ROWS, :, :].rearrange("p g n -> p (g n)"), MAX_UNIT).then_inc(consts_ready, 1)
            pool.wait_ge(consts_ready, 6)

            def power(which, count, i):
                pool.wait_ge(var_ready[which], count)
                pool.tensor_tensor(rstd[:, i:i + 1], vpe[:, i:i + 1], neg_half, ALU.pow).then_inc(rstd_ready[which], 1)

            def weight_max(n):
                pool.wait_ge(wabs_ready, n + 1)
                pool.partition_all_reduce(wall[:, n:n + 1], wabs[:, n:n + 1], P,
                                          bass.bass_isa.ReduceOp.max).then_inc(wall_ready, 1)

            for n in range(TT):
                power(0, n + 1, n % 2)
                if n < 2:
                    weight_max(n)
            weight_max(2)
            weight_max(3)

            def batch(b):
                for ev in events_of(b):
                    kind, i = ev
                    if kind == "LN":
                        power(0, (b + 1) * TT + i + 1, i % 2)
                    elif kind == "R" and i % 2 == 0:
                        power(1, owner(b, ev) * 2 * TT + i // 2 + 1, 2 + i % 4 // 2)
                    elif kind == "S" and MASKED[i]:
                        wait_free(pool, b, ev)
                        settle(pool)
                        for x, (t, _, j) in enumerate(S_UNITS[i]):
                            if j == t:
                                d = p32[:, i % PB, 512 * x:512 * x + 512].rearrange("p (h n) -> p h n", h=NREP)
                                ins = pool.affine_select(out=d, in_=d, compare_op=ALU.is_ge, fill=0.0, base=0,
                                                         pattern=[[0, NREP], [1, P]], channel_multiplier=-1)
                        ins.then_inc(p_masked, 1)

            over_batches(pool, batch)
            power(1, NB * 2 * TT, 3)
            pool.sem_inc(tmp_free, RT)
            pool.wait_ge(wide_full, NB * NW)
            pool.memset(acc.rearrange("p o n -> p (o n)"), 0.0).then_inc(acc_zero, 1)
            pool.wait_ge(acc_zero, 1)

            def tile(n, par):
                units = unit_list(n)
                for u, number, buf in pool_units(n):
                    o, c = u[1] // 2, u[1] % 2
                    unit_done(pool, units, u)
                    pool.wait_ge(tmp_free, RT + number - 1)
                    a = acc[:, o, c * HALF:c * HALF + HALF]
                    pool.tensor_tensor(a, tmp[:, buf, :], a, ALU.add).then_inc(tmp_free, 1)

            over_tiles(pool, tile)
            tile(NT, 0)
            for f in range(NF):
                pool.wait_ge(fvar_ready, f + 1)
                pool.tensor_tensor(rstd[:, f % 2:f % 2 + 1], vpe[:, f % 2:f % 2 + 1], neg_half,
                                   ALU.pow).then_inc(frstd_ready, 1)

        @block.scalar
        def _(act):
            w_hi = [w_k[:, 0], w_v[:, 0], w_q[:, 0], w_o[:, 0]]
            stages = [stage_k, stage_v, stage_q, stage_o]

            def weight_hi(n):
                act.wait_ge(wfac_ready, n + 1)
                act.activation(w_hi[n], stages[n], ACT.Copy, scale=wfac[:, n:n + 1]).then_inc(whi_ready, 1)

            def probabilities_hi(b, u):
                if MASKED[u]:
                    act.wait_ge(p_masked, b * NM + sum(MASKED[0:u + 1]))
                else:
                    wait_free(act, b, ("S", u))
                wait(act, pv_done, b * NS + u - PB + 1)
                act.activation(p_hl[:, u % PB, 0, :], p32[:, u % PB, :], ACT.Copy).then_inc(phi_ready, 1)

            def split_hi(b, ev):
                kind, i = ev
                if kind == "K" and i == 0:
                    wait(act, qs_stacked[1], b * 384)
                    if is_first(b):
                        act.wait_ge(wlo_ready, 2)
                elif kind == "Q" and i % 2 == 0:
                    if i == 0:
                        wait(act, qs_stacked[0], b * 384)
                    elif i == 2:
                        act.wait_ge(ks_stacked, (b + 1) * 192)
                    else:
                        act.wait_ge(qs_stacked[i // 2 % 2], b * 384 + 192)
                elif kind == "V" and is_first(b):
                    act.wait_ge(consts_ready, 6)
                elif kind == "T1":
                    wait(act, plo_ready, b * NS)
                elif kind == "T2" and i >= 2:
                    act.wait_ge(wide_full, b * NW + WIDE[("WO", i - 2)] + 1)
                elif kind == "T3":
                    wait(act, x2t_stored, b * TT * 16 + i * 16)
                if ev in WIDE:
                    act.wait_ge(wide_full, b * NW + WIDE[ev] + 1)
                else:
                    wait_full(act, b, ev)
                src, hi, _ = split_views(b, ev)
                act.activation(hi, src, ACT.Copy).then_inc(hi_ready, 1)

            def batch(b):
                for ev in events_of(b):
                    kind, i = ev
                    if is_first(b) and ev == ("Q", 0):
                        weight_hi(2)
                    if is_first(b) and ev == ("V", 0):
                        weight_hi(3)
                    if kind in SPLIT:
                        split_hi(owner(b, ev), ev)
                    elif kind == "S":
                        if is_first(b) and i == 0:
                            act.wait_ge(wlo_ready, 4)
                            act.wait_ge(scales_ready, 1)
                        wait_full(act, b, ev)
                        wait(act, plo_ready, b * NS + i - PB + 1)
                        free(act.activation(p32[:, i % PB, :], slot(b, ev), ACT.Exp, scale=score_f[:, 0:1]), b, ev)
                        if i >= 1:
                            probabilities_hi(b, i - 1)
                    elif ev == ("END", 0):
                        probabilities_hi(b, NS - 1)
                    elif kind == "MT":
                        act.wait_ge(wide_full, b * NW + WIDE[ev] + 1)
                        wait(act, mrow_loaded, b * 64 + 32 * i)
                        first, end = head_range(i)
                        act.activation(mrow[0:end - first, 0, :], wide_bank(ev)[0:end - first, :], ACT.Copy,
                                       scale=-1.0 / MAX_UNIT).then_inc(hi_ready, 1)

            weight_hi(0)
            weight_hi(1)
            for ev in prologue:
                if ev[0] == "T1":
                    split_hi(0, ev)
            over_batches(act, batch)

            def convert_gu(n, par):
                act.wait_ge(gu_loaded, (n + 1) * 16)
                act.activation(w_gu[:, par].rearrange("p w k n -> p (w k n)"), int_gu, ACT.Copy).then_inc(gu_conv, 1)

            def convert_d(n, par):
                act.wait_ge(d_loaded, (n + 1) * 16)
                act.wait_ge(gusc_ready, n + 1)
                act.activation(w_d[:, par, :], int_d, ACT.Copy, scale=gu_sc[:, par, 24:25]).then_inc(d_conv, 1)

            split_hi(NB - 1, ("T3", TT - 1))
            act.wait_ge(x1_stored[0], 32 * NB)
            act.wait_ge(x1_stored[1], 32 * NB)
            act.wait_ge(x2t_stored, 16 * NB * TT)
            convert_gu(0, 0)

            def down_unit(par, units, u, number, buf):
                o = u[1] // 2
                unit_filled(act, units, u)
                act.wait_ge(tmp_free, number + 1)
                act.activation(tmp[:, buf, :], ffn_slot[units[u][0]], ACT.Copy,
                               scale=dn_sc[:, par if u[0] == "c" else 1 - par, o:o + 1])\
                    .then_inc(unit_free[units[u][0]], 1)

            def tile(n, par):
                units = unit_list(n)
                down = {u: (number, buf) for u, number, buf in pool_units(n)}
                seen_d = False
                for u in units:
                    kind, j = u
                    if kind == "g":
                        w, g, c = gu_parts(j)
                        if j in AT_HI and not (isinstance(n, int) and n == 0):
                            hidden_hi(n - 1, 1 - par, AT_HI.index(j))
                        if g == 0:
                            unit_filled(act, units, u)
                            act.wait_ge(gusc_ready, n + 1)
                            if w == 0:
                                dst = gacc[:, par, c * HALF:c * HALF + HALF]
                            else:
                                wait(act, h_ready, n * 2)
                                dst = uacc[:, c * HALF:c * HALF + HALF]
                            act.activation(dst, ffn_slot[units[u][0]], ACT.Copy,
                                           scale=gu_sc[:, par, 8 * w:8 * w + 1]).then_inc(unit_free[units[u][0]], 1)
                        if j in (20, 21):
                            unit_done(act, units, ("g", j - 6))
                            ga = gacc[:, par, (j - 20) * HALF:(j - 20) * HALF + HALF]
                            act.activation(ga, ga, ACT.Silu).then_inc(silu_done, 1)
                        if j == 10:
                            if ("c", DN - 1) in units:
                                unit_filled(act, units, ("c", DN - 1))
                            convert_d(n, par)
                        if j == 25 and not (isinstance(n, int) and n == NT - 1):
                            convert_gu(n + 1, 1 - par)
                    elif u in down:
                        if kind == "d" and not seen_d:
                            act.wait_ge(dnsc_ready, n)
                            seen_d = True
                        down_unit(par, units, u, *down[u])

            def hidden_hi(m, par, c):
                act.wait_ge(h32_ready, m * 2 + c + 1)
                act.activation(hid[:, par, 0, c * HALF:c * HALF + HALF], uacc[:, c * HALF:c * HALF + HALF],
                               ACT.Copy).then_inc(hhi_ready, 1)

            over_tiles(act, tile)
            units = unit_list(NT)
            for c in range(2):
                hidden_hi(NT - 1, 1, c)
            act.wait_ge(dnsc_ready, NT)
            for u, number, buf in pool_units(NT):
                down_unit(0, units, u, number, buf)
            for f in range(NF):
                act.wait_ge(fnmr_ready, f + 1)
                if f >= 4:
                    act.wait_ge(out_stored[f % 4], 16 * (f // 4))
                act.activation(y_t[:, f % 4, :], ffn_slot[f % 4], ACT.Identity, bias=rs2[:, f % 2:f % 2 + 1],
                               scale=rstd[:, f % 2:f % 2 + 1]).then_inc(unit_free[f % 4], 1)

        @block.vector
        def _(dve):
            steps = {"base": 0, "n": 0}

            def link(ins):
                ins.then_inc(dve_step, 1)
                steps["n"] += 1
                dve.wait_ge(dve_step, steps["base"] + steps["n"])

            def variance(halves, i, fac=None):
                for k in range(2):
                    ins = dve.bn_stats(stats[:, i, 6 * k:6 * k + 6], halves[k])
                link(ins)
                settle(dve)
                link(dve.bn_aggr(mv[:, i, :], stats[:, i, :]))
                src = mv[:, i, 1:2]
                if fac is not None:
                    link(dve.tensor_scalar(vpe[:, i:i + 1], src, fac, fac, ALU.mult, ALU.mult))
                    src = vpe[:, i:i + 1]
                return dve.tensor_scalar(vpe[:, i:i + 1], src, EPS, None, ALU.add)

            w_stage = [stage_k, stage_v, stage_q, stage_o]
            w_hl = [w_k, w_v, w_q, w_o]

            def weight_factor(n):
                dve.wait_ge(w_loaded[n], 16)
                dve.tensor_reduce(wabs[:, n:n + 1], w_stage[n].rearrange("p k n -> p (k n)"), AX.X, ALU.max,
                                  apply_absolute_value=True).then_inc(wabs_ready, 1)
                dve.wait_ge(wall_ready, n + 1)
                power_of_two(wpow[:, n:n + 1], wall[:, n:n + 1])
                link(dve.tensor_scalar(wall[:, n:n + 1], wpow[:, n:n + 1], 0.5, None, ALU.mult))
                dve.reciprocal(wfac[:, n:n + 1], wall[:, n:n + 1]).then_inc(wfac_ready, 1)

            def power_of_two(dst, src):
                link(dve.tensor_scalar(dst, src, 1e-30, 1e30, ALU.max, ALU.min))
                link(dve.tensor_scalar(dst.bitcast(I32), dst.bitcast(I32), 0x7F800000, None, ALU.bitwise_and))

            def weight_lo(n):
                dve.wait_ge(whi_ready, n + 1)
                flat = "p k n -> p (k n)"
                dve.scalar_tensor_tensor(out=w_hl[n][:, 1].rearrange(flat), in0=w_stage[n].rearrange(flat),
                                         scalar=wfac[:, n:n + 1], in1=w_hl[n][:, 0].rearrange(flat),
                                         op0=ALU.mult, op1=ALU.subtract).then_inc(wlo_ready, 1)

            def scale_tables():
                dve.wait_ge(s_loaded, 16)
                link(dve.tensor_scalar(score_f, wpow[:, 0:1], wpow[:, 2:3], 0.25 * HD ** -0.5, ALU.mult, ALU.mult))
                link(dve.tensor_scalar(out_f, wpow[:, 1:2], wpow[:, 3:4], 0.25, ALU.mult, ALU.mult))
                inv = all_scales[:, :, 24:25]
                dve.wait_ge(wlo_ready, 4)
                low = stage_o[:, 0, 0:NT].rearrange("p (n c) -> p n c", c=1)
                link(dve.tensor_reduce(inv, all_scales[:, :, 0:8], AX.X, ALU.max, apply_absolute_value=True))
                link(dve.tensor_reduce(low, all_scales[:, :, 8:16], AX.X, ALU.max, apply_absolute_value=True))
                link(dve.tensor_tensor(inv, inv, low, ALU.mult))
                power_of_two(inv, inv)
                link(dve.tensor_scalar(inv, inv, 4096.0, None, ALU.mult))
                link(dve.reciprocal(low, inv))
                up = all_scales[:, :, 8:16]
                dve.tensor_tensor(up, up, low.broadcast_to([P, NT, 8]), ALU.mult).then_inc(scales_ready, 1)

            def input_variance(b, t):
                dve.wait_ge(x_loaded[t % XB], (b * X_LOADS[t % XB] + t // XB + 1) * 16)
                tile = xin[:, t % XB, :]
                variance([tile[:, 0:512], tile[:, 512:1024]], t % 2).then_inc(var_ready[0], 1)

            def input_normal(b, t):
                tile = xin[:, t % XB, :]
                dve.wait_ge(rstd_ready[0], b * TT + t + 1)
                dve.tensor_scalar(tile, tile, mv[:, t % 2, 0:1], rstd[:, t % 2:t % 2 + 1], ALU.subtract,
                                  ALU.mult).then_inc(xn_ready[0], 1)

            def hi_written(b, ev):
                before, n = HIS.of(b, ev)
                dve.wait_ge(hi_ready, before * HIS.per + n + 1)

            def split_lo(b, ev):
                hi_written(b, ev)
                src, hi, lo = split_views(b, ev)
                ins = dve.tensor_tensor(lo, src, hi, ALU.subtract)
                if ev in WIDE:
                    ins.then_inc(wide_free, 1)
                else:
                    free(ins, b, ev)

            def maxima(b, ev):
                wait_full(dve, b, ev)
                settle(dve)
                for h, t, at in max_parts(ev):
                    n = P * (t + 1)
                    sc = slot(b, ev)[:, at:at + n]
                    ins = dve.tensor_tensor_reduce(
                        out=sc, in0=sc, in1=mask[:, S - n:S], scale=1.0, scalar=NEG, op0=ALU.add, op1=ALU.max,
                        accum_out=mcol[:, t, h:h + 1])
                free(ins, b, ev)

            def probabilities_lo(b, u):
                dve.wait_ge(phi_ready, b * NS + u + 1)
                dve.tensor_tensor(p_hl[:, u % PB, 1, :], p32[:, u % PB, :], p_hl[:, u % PB, 0, :],
                                  ALU.subtract).then_inc(plo_ready, 1)

            def normalise(b, u):
                t, g, j = S_UNITS[u][-1]
                if j < t or GROUP_NO[t, g] % 2 == 0:
                    return
                n = GROUP_NO[t, g] // 2
                dve.wait_ge(pv_done, b * NS + u + 1)
                o = pv_ps[n % 2].rearrange("p (h d) -> p h d", h=2 * NREP)
                wait(dve, pv_free, b * NG2 + n - 1)
                r = rsum[:, n % 2]
                link(dve.reciprocal(r, o[:, :, HD:HD + 1]))
                dve.tensor_tensor(attn[:, t % 2, P * (g - 1):P * g + P].rearrange("p (h d) -> p h d", h=2 * NREP),
                                  o[:, :, 0:HD], r.broadcast_to([P, 2 * NREP, HD]), ALU.mult).then_inc(pv_free, 1)

            def residual(b, t, step):
                y, r = wide_ps, xr[:, t % 2, :]
                if step == 0:
                    dve.wait_ge(wide_full, b * NW + WIDE[("WO", t)] + 1)
                    variance([y[:, 0:512], y[:, 512:1024]], 2, out_f).then_inc(var_ready[1], 1)
                elif step == 1:
                    dve.wait_ge(rstd_ready[1], b * 2 * TT + 2 * t + 1)
                    link(dve.tensor_scalar(rs2[:, 0:1], rstd[:, 2:3], out_f, None, ALU.mult))
                    dve.tensor_scalar(xb, y, mv[:, 2, 0:1], rs2[:, 0:1], ALU.subtract, ALU.mult).then_inc(wide_free, 1)
                elif step == 2:
                    dve.wait_ge(wide_free, b * NW + WIDE[("WO", t)] + 1)
                    dve.wait_ge(xr_loaded[t % 2], b * 32 + (t // 2 + 1) * 16)
                    dve.tensor_tensor(r, r, xb, ALU.add).then_inc(x1_ready, 1)
                    dve.wait_ge(x1_ready, b * TT + t + 1)
                    variance([r[:, 0:512], r[:, 512:1024]], 3).then_inc(var_ready[1], 1)
                else:
                    dve.wait_ge(rstd_ready[1], b * 2 * TT + 2 * t + 2)
                    dve.tensor_scalar(xb, r, mv[:, 3, 0:1], rstd[:, 3:4], ALU.subtract, ALU.mult).then_inc(xn_ready[1], 1)

            def attention_step(b, ev):
                    kind, i = ev
                    if is_first(b) and ev == ("Q", 0):
                        weight_factor(2)
                        weight_lo(2)
                    if is_first(b) and ev == ("V", 0):
                        weight_factor(3)
                        weight_lo(3)
                        scale_tables()
                    if kind in SPLIT:
                        split_lo(owner(b, ev), ev)
                    elif kind in ("MA", "MB"):
                        maxima(b, ev)
                    elif kind == "S" and i >= 1:
                        probabilities_lo(b, i - 1)
                    elif ev == ("END", 0):
                        probabilities_lo(b, NS - 1)
                    elif ev == ("END", 1):
                        normalise(b, NS - 1)
                    elif kind == "PV" and i >= 1:
                        normalise(b, i - 1)
                    elif kind == "MT":
                        hi_written(b, ev)
                        first, end = head_range(i)
                        dve.scalar_tensor_tensor(out=mrow[0:end - first, 1, :], in0=wide_bank(ev)[0:end - first, :],
                                                 scalar=-1.0 / MAX_UNIT, in1=mrow[0:end - first, 0, :], op0=ALU.mult,
                                                 op1=ALU.subtract).then_inc(wide_free, 1)
                    elif kind == "R":
                        residual(owner(b, ev), i // 4, i % 4)
                    elif kind == "LN":
                        input_variance(b + 1, i)
                    elif kind == "LX":
                        input_normal(b + 1, i)

            def batch(b):
                for ev in events_of(b):
                    attention_step(b, ev)

            dve.wait_ge(consts_ready, 3)
            for ev in prologue:
                if ev[0] == "LN":
                    input_variance(0, ev[1])
                    input_normal(0, ev[1])
                    if ev[1] < 2:
                        weight_factor(ev[1])
                        if ev[1] == 1:
                            weight_lo(0)
                            weight_lo(1)
                else:
                    split_lo(0, ev)
            batch(0)
            per, first_steps = TT * 2 + NG2 + TT * 6, steps["n"]
            with dve.Fori(1, NB - 1) as b:
                steps["base"], steps["n"] = b * per + (first_steps - per), 0
                batch(b)
                assert steps["n"] == per, steps["n"]
            steps["base"], steps["n"] = (NB - 2) * per + first_steps, 0
            batch(NB - 1)
            for ev in epilogue:
                attention_step(NB, ev)

            def tile(n, par):
                first = isinstance(n, int) and n == 0
                units = unit_list(n)
                if first:
                    dve.tensor_copy(gu_sc[:, 0, :], all_scales[:, 0, :]).then_inc(gusc_ready, 1)
                for u in units:
                    kind, j = u
                    ps = ffn_slot[units[u][0]]
                    done = unit_free[units[u][0]]
                    if kind == "g":
                        w, g, c = gu_parts(j)
                        if j in AT_H and not first:
                            hidden(n - 1, 1 - par, unit_list(n - 1), AT_H.index(j))
                        if j in AT_LO and not first:
                            hidden_lo(n - 1, 1 - par, AT_LO.index(j))
                        if g > 0:
                            unit_filled(dve, units, u)
                            unit_done(dve, units, ("g", j - 2))
                            a = (gacc[:, par] if w == 0 else uacc)[:, c * HALF:c * HALF + HALF]
                            dve.scalar_tensor_tensor(out=a, in0=ps, scalar=gu_sc[:, par, 8 * w + g:8 * w + g + 1],
                                                     in1=a, op0=ALU.mult, op1=ALU.add).then_inc(done, 1)
                        if j == 12 and not (isinstance(n, int) and n == NT - 1):
                            wait(dve, d_conv, n)
                            dve.tensor_copy(gu_sc[:, 1 - par, :], all_scales[:, n + 1, :]).then_inc(gusc_ready, 1)
                    elif j in DVE_D:
                        down_unit(n, par, units, u)
                carried = [u for u in units if u[0] == "c" and u[1] not in DVE_D]
                if carried:
                    unit_done(dve, units, carried[-1])
                dve.tensor_copy(dn_sc[:, par, :], all_scales[:, n, 16:24]).then_inc(dnsc_ready, 1)
            def hidden(m, par, units, c):
                unit_done(dve, units, ("g", GU - 2 + c))
                dve.wait_ge(silu_done, m * 2 + c + 1)
                ua = uacc[:, c * HALF:c * HALF + HALF]
                dve.tensor_tensor(ua, ua, gacc[:, par, c * HALF:c * HALF + HALF], ALU.mult).then_inc(h32_ready, 1)

            def hidden_lo(m, par, c):
                dve.wait_ge(hhi_ready, m * 2 + c + 1)
                dve.tensor_tensor(hid[:, par, 1, c * HALF:c * HALF + HALF], uacc[:, c * HALF:c * HALF + HALF],
                                  hid[:, par, 0, c * HALF:c * HALF + HALF], ALU.subtract).then_inc(h_ready, 1)

            def down_unit(n, par, units, u):
                o, c = u[1] // 2, u[1] % 2
                unit_filled(dve, units, u)
                dve.wait_ge(dnsc_ready, n)
                a = acc[:, o, c * HALF:c * HALF + HALF]
                dve.scalar_tensor_tensor(out=a, in0=ffn_slot[units[u][0]], scalar=dn_sc[:, par if u[0] == "c" else 1 - par, o:o + 1], in1=a,
                                         op0=ALU.mult, op1=ALU.add).then_inc(unit_free[units[u][0]], 1)

            dve.wait_ge(acc_zero, 1)
            over_tiles(dve, tile)
            for c in range(2):
                hidden(NT - 1, 1, unit_list(NT - 1), c)
            for c in range(2):
                hidden_lo(NT - 1, 1, c)
            units = unit_list(NT)
            for u in units:
                if u[1] in DVE_D:
                    down_unit(NT, 0, units, u)

            for f in range(NF + 2):
                if f < NF:
                    i = f % 2
                    y = ffn_slot[f % 4]
                    dve.wait_ge(unit_full[f % 4], F0 + f // 4 + 1)
                    if f >= 2:
                        dve.wait_ge(unit_free[(f - 2) % 4], F0 + (f - 2) // 4 + 1)
                    variance([y[:, 0:512], y[:, 512:1024]], i).then_inc(fvar_ready, 1)
                if 1 <= f <= NF:
                    i = (f - 1) % 2
                    dve.wait_ge(frstd_ready, f)
                    dve.tensor_scalar(rs2[:, i:i + 1], mv[:, i, 0:1], rstd[:, i:i + 1], -1.0, ALU.mult,
                                      ALU.mult).then_inc(fnmr_ready, 1)
                if f >= 2:
                    g = f - 2
                    dve.wait_ge(unit_free[g % 4], F0 + g // 4 + 1)
                    dve.wait_ge(x1b_loaded[g % 4], 16 * (g // 4 + 1))
                    dve.tensor_tensor(y_t[:, g % 4, :], y_t[:, g % 4, :], x1_b[:, g % 4, :],
                                      ALU.add).then_inc(out_ready, 1)

        @block.tensor
        def _(pe):
            PAIRS = ((0, 0), (0, 1), (1, 0))

            def transposes(dst, src, n, width=P):
                for k in range(n):
                    ins = pe.transpose(dst(k), src(k), ident)
                return ins

            def enter(b, ev):
                s, n = slot_number(b, ev)
                wait(pe, slot_free[s], n)

            def projection(b, job, piece):
                kind, i = job
                dst = wide_bank(job)
                if kind == "V":
                    t, ks = piece // 2, range(KD // 2 * (piece % 2), KD // 2 * (piece % 2) + KD // 2)
                    tok = P * (2 * i + t)
                    dst = dst[:, 256 * t:256 * t + 256]
                    terms = lambda a, c, k: (xnt[:, a, k, tok:tok + P], w_v[:, c, k, :])
                else:
                    w = w_k if kind == "K" else w_q
                    ks = range(KD // 4 * piece, KD // 4 * piece + KD // 4)
                    terms = lambda a, c, k: (w[:, a, k, P * i:P * i + P], xnt[:, c, k, :])
                for k in ks:
                    for m, (a, c) in enumerate(PAIRS):
                        lhs, rhs = terms(a, c, k)
                        ins = pe.matmul(dst, lhs, rhs, start=(k == 0 and m == 0), stop=(k == KD - 1 and m == 2))
                if piece == 3:
                    ins.then_inc(wide_full, 1)

            def input_transposes(b, t):
                ev = ("T1", t)
                enter(b, ev)
                pe.wait_ge(xn_ready[0], b * TT + t + 1)
                full(transposes(lambda k: slot(b, ev)[:, P * k:P * k + P],
                                lambda k: xin[:, t % XB, P * k:P * k + P], KD), b, ev)

            def residual_transposes(b, t):
                ev = ("T3", t)
                enter(b, ev)
                wait(pe, xn_ready[1], b * TT + t + 1)
                full(transposes(lambda k: slot(b, ev)[:, P * k:P * k + P], lambda k: xb[:, P * k:P * k + P], KD), b, ev)

            def batch(b):
                for ev in events_of(b):
                    kind, i = ev
                    if kind == "T1":
                        input_transposes(b + 1, i)
                        continue
                    if kind == "T3":
                        residual_transposes(owner(b, ev), i)
                        continue
                    if kind in SLOT_KINDS:
                        enter(b, ev)
                    if kind == "PP":
                        job, piece = i
                        if piece == 0:
                            wide_wait(pe, b, job)
                            if job == ("K", 0):
                                wait_free(pe, b, ("T1", TT - 1))
                            if is_first(b) and job in (("K", 0), ("Q", 0)):
                                pe.wait_ge(wlo_ready, 2 if job[0] == "K" else 3)
                        projection(b, job, piece)
                    elif kind in ("MA", "MB"):
                        if kind == "MA" and i % 8 == 0:
                            u = i // 8
                            pe.wait_ge(ks_stacked, (b + 1) * 192)
                            pe.wait_ge(qs_stacked[u % 2], b * 384 + (u // 2 + 1) * 192)
                        for h, t, at in max_parts(ev):
                            n = P * (t + 1)
                            ins = pe.matmul(slot(b, ev)[:, at:at + n], q_s[0:3 * HD, h, P * t:P * t + P],
                                            k_s[0:3 * HD, h // NREP, 0:n], start=True, stop=True)
                        full(ins, b, ev)
                    elif kind == "MT":
                        wide_wait(pe, b, ev)
                        first, end = head_range(i)
                        wait_free(pe, b, ("MB", end // 2 - 1))
                        transposes(lambda t: wide_bank(ev)[0:end - first, P * t:P * t + P],
                                   lambda t: mcol[:, t, first:end], TT).then_inc(wide_full, 1)
                    elif kind == "S":
                        if i in (0, LATE_UNIT):
                            pe.wait_ge(mrow_loaded, b * 64 + (32 if i == 0 else 64))
                        for x, (t, g, j) in enumerate(S_UNITS[i]):
                            ins = pe.matmul(slot(b, ev)[:, 512 * x:512 * x + 512],
                                            k_s[0:SOFTMAX_ROWS, g, P * j:P * j + P],
                                            q_s[0:SOFTMAX_ROWS, NREP * g:NREP * g + NREP, P * t:P * t + P],
                                            start=True, stop=True)
                        full(ins, b, ev)
                    elif kind == "PV":
                        pe.wait_ge(plo_ready, b * NS + i + 1)
                        for x, (t, g, j) in enumerate(S_UNITS[i]):
                            n, second = GROUP_NO[t, g] // 2, GROUP_NO[t, g] % 2
                            if j == 0 and not second:
                                wait(pe, pv_free, b * NG2 + n - 1)
                            for r in range(NREP):
                                at = 33 * (NREP * second + r)
                                dst = pv_ps[n % 2][:, at:at + 33]
                                cols = slice(512 * x + P * r, 512 * x + P * r + P)
                                hi, lo = p_hl[:, i % PB, 0, cols], p_hl[:, i % PB, 1, cols]
                                pe.matmul(dst, hi, v_a[:, j, g, :], start=(j + r + second == 0), stop=False,
                                          skip_group_check=True)
                                pe.matmul(dst, hi, v_b[:, j, g, :], start=False, stop=False, skip_group_check=True)
                                ins = pe.matmul(dst, lo, v_a[:, j, g, :], start=False, stop=(j == t and r == NREP - 1 and second == 1),
                                                skip_group_check=True)
                        ins.then_inc(pv_done, 1)
                    elif kind == "T2":
                        pe.wait_ge(pv_free, b * NG2 + GROUP_NO[i, NKV - 1] // 2 + 1)
                        full(transposes(lambda k: slot(b, ev)[:, P * k:P * k + P],
                                        lambda k: attn[:, i % 2, P * k:P * k + P], KD), b, ev)
                    elif kind == "WP":
                        t, m, k0 = i // 8, i % 8 // 4, i % 4 * 2
                        if i % 8 == 0:
                            wide_wait(pe, b, ("WO", t))
                            wait_free(pe, b, ("T2", t))
                        for k in (k0, k0 + 1):
                            for n, (a, c) in enumerate(PAIRS):
                                ins = pe.matmul(wide_ps[:, 512 * m:512 * m + 512], at_t[:, t % 2, a, k, :],
                                                w_o[:, c, k, 512 * m:512 * m + 512], start=(k == 0 and n == 0),
                                                stop=(k == KD - 1 and n == 2))
                        if i % 8 == 7:
                            ins.then_inc(wide_full, 1)

            pe.wait_ge(ident_ready, 2)
            for ev in prologue:
                if ev[0] == "T1":
                    input_transposes(0, ev[1])
            over_batches(pe, batch)
            residual_transposes(NB - 1, TT - 1)
            wait_free(pe, NB - 1, ("T3", TT - 2))
            wait_free(pe, NB - 1, ("T3", TT - 1))
            pe.wait_ge(wide_free, NB * NW)
            pe.wait_ge(pv_free, NB * NG2)

            def gu_unit(n, par, units, u):
                w, g, c = gu_parts(u[1])
                s, _ = units[u]
                for m in range(2):
                    b = 2 * c + m
                    for hl in range(2):
                        ins = pe.matmul(ffn_slot[s][:, S * m:S * m + S], w_gu[:, par, w, g, :], xt[:, TT * b:TT * b + TT, hl, g, :],
                                        start=(hl == 0), stop=(hl == 1))
                ins.then_inc(unit_full[s], 1)

            def down_unit(n, par, units, u):
                o, c = u[1] // 2, u[1] % 2
                dpar = par if u[0] == "c" else 1 - par
                s, _ = units[u]
                for m in range(2):
                    at = c * HALF + S * m
                    for hl in range(2):
                        ins = pe.matmul(ffn_slot[s][:, S * m:S * m + S], w_d[:, dpar, P * o:P * o + P],
                                        hid[:, dpar, hl, at:at + S], start=(hl == 0), stop=(hl == 1))
                ins.then_inc(unit_full[s], 1)

            def tile(n, par):
                units = unit_list(n)
                first_d = True
                for u in units:
                    s, before = units[u]
                    wait(pe, unit_free[s], before)
                    if u[0] == "g":
                        if u[1] == 0:
                            pe.wait_ge(gu_conv, n + 1)
                        if isinstance(n, int) and n == 0 and u[1] < 2:
                            pe.wait_ge(xt_loaded[2 * u[1]], 16)
                            pe.wait_ge(xt_loaded[2 * u[1] + 1], 16)
                        gu_unit(n, par, units, u)
                    else:
                        if u[0] == "d" and first_d:
                            pe.wait_ge(d_conv, n)
                            pe.wait_ge(h_ready, n * 2)
                            first_d = False
                        down_unit(n, par, units, u)

            over_tiles(pe, tile)
            tile(NT, NT % 2)
            lasts = unit_list(NT)
            half_pool = [[number for u, number, _ in pool_units(NT) if u[0] == "c" or u[1] % 2 <= c][-1] for c in range(2)]
            half_dve = [[u for u in lasts if u[0] == "d" and u[1] % 2 == c and u[1] in DVE_D][-1:] for c in range(2)]
            for f in range(NF):
                c = f // (NF // 2)
                if f % (NF // 2) == 0:
                    pe.wait_ge(tmp_free, RT + half_pool[c] + 1)
                    for u in half_dve[c]:
                        unit_done(pe, lasts, u)
                pe.wait_ge(unit_free[f % 4], F0 + f // 4)
                for k in range(KD):
                    ins = pe.transpose(ffn_slot[f % 4][:, P * k:P * k + P], acc[:, k, f * P:f * P + P], ident)
                ins.then_inc(unit_full[f % 4], 1)


_SHAPES = [((4, 512, 1024), "float32")]


def kernel(L0_attn_x, L0_attn_wq, L0_attn_wk, L0_attn_wv, L0_attn_wo, L0_ffn_gate_q, L0_ffn_gate_s,
           L0_ffn_up_q, L0_ffn_up_s, L0_ffn_down_q, L0_ffn_down_s):
    import numpy as np
    import concourse.bacc as bacc
    from concourse import mybir as mb
    from concourse.bass_utils import run_bass_kernel_spmd

    p = 128
    x = np.asarray(L0_attn_x)
    gate, up, down = (np.asarray(a) for a in (L0_ffn_gate_q, L0_ffn_up_q, L0_ffn_down_q))
    gate_s, up_s, down_s = (np.asarray(a) for a in (L0_ffn_gate_s, L0_ffn_up_s, L0_ffn_down_s))
    inter, width = gate.shape
    nt, kd = inter // p, width // p
    gu = np.stack([gate, up]).reshape(2, nt, p, kd, p).transpose(1, 4, 0, 3, 2).reshape(nt, p, 2 * kd * p)
    dn = down.reshape(width, nt, p).transpose(1, 2, 0)
    sc = np.concatenate([gate_s.reshape(nt, p, kd), up_s.reshape(nt, p, kd),
                         down_s.reshape(kd, p, nt).transpose(2, 1, 0)], axis=2)
    arrays = {"x": x, "wq": L0_attn_wq, "wk": L0_attn_wk, "wv": L0_attn_wv, "wo": L0_attn_wo,
              "gu_t": gu, "down_t": dn, "scales": sc}
    arrays = {k: np.ascontiguousarray(v) for k, v in arrays.items()}

    nc = bacc.Bacc("TRN2", target_bir_lowering=False, num_devices=1)
    aps = {k: nc.dram_tensor(f"in_{k}", v.shape, mb.dt.from_np(v.dtype), kind="ExternalInput").ap()
           for k, v in arrays.items()}
    out = nc.dram_tensor("out_0", (x.shape[0] * x.shape[1], x.shape[2]), mb.dt.float32, kind="ExternalOutput").ap()
    sandwich(nc, out=out, **aps)
    r = run_bass_kernel_spmd(nc, [{f"in_{k}": v for k, v in arrays.items()}], core_ids=[0])
    return r.results[0]["out_0"].reshape(x.shape)
```

```python
from contextlib import ExitStack

import concourse.bass as bass
from concourse import mybir

F32 = mybir.dt.float32
F16 = mybir.dt.float16
BF16 = mybir.dt.bfloat16
I32 = mybir.dt.int32
ALU = mybir.AluOpType
ACT = mybir.ActivationFunctionType
AX = mybir.AxisListType

P = 128
HD = 32
SOFTMAX_ROWS = 98
MAX_UNIT = 32768.0


def sandwich(nc, x, wq, wk, wv, wo, gu_t, down_t, scales, out):
    NB, S, D = x.shape
    NH = wq.shape[1] // HD
    NKV = wk.shape[1] // HD
    NREP = NH // NKV
    KD = D // P
    TT = S // P
    NT = gu_t.shape[0]
    NTOK = NB * S
    HALF = 2 * S
    NU = NH // 8
    EPS = 1e-5
    assert HD * NREP == P and KD == 8 and TT == 4 and S == 512 and NB == 4 and NKV == 8

    x1_scr = nc.dram_tensor("x1_scratch", [NB, TT, P, D], F32, kind="Internal").ap()
    xt_scr = nc.dram_tensor("xt_scratch", [NB, TT, P, 2 * KD * P], F16, kind="Internal").ap()

    NEG = -1.0e30
    EARLY = NKV - 2
    GROUPS = [(t, g) for t in (0, 1) for g in range(EARLY)] + [(t, g) for t in (0, 1) for g in range(EARLY, NKV)]
    GROUPS += [(t, g) for t in range(2, TT) for g in range(NKV)]
    GROUP_NO = {tg: n for n, tg in enumerate(GROUPS)}
    NG2 = len(GROUPS) // 2
    banks = [(t, g, j) for t, g in GROUPS for j in range(t + 1)]
    S_UNITS = [banks[i:i + 2] for i in range(0, len(banks), 2)]
    NS = len(S_UNITS)
    MASKED = [any(j == t for t, _, j in u) for u in S_UNITS]
    NM = sum(MASKED)
    assert all(GROUPS[n + 1] == (GROUPS[n][0], GROUPS[n][1] + 1) for n in range(0, len(GROUPS), 2))
    LATE_UNIT = [any(g >= EARLY for _, g, _ in u) for u in S_UNITS].index(True)
    PB = 4
    LAG = 3

    with ExitStack() as ctx:
        ARENA = 53200
        arena = ctx.enter_context(nc.sbuf_tensor("arena", [P, ARENA], F32))
        place = {"at": 0}

        def carve(words, dtype=F32, at=None):
            if at is None:
                at = place["at"]
                place["at"] = at + words
                assert place["at"] <= ARENA, place["at"]
            v = arena[:, at:at + words]
            return v if dtype == F32 else v.bitcast(dtype)

        ident = carve(P)
        all_scales = carve(NT * 25).rearrange("p (n c) -> p n c", n=NT)
        gu_sc = carve(2 * 25).rearrange("p (b c) -> p b c", b=2)
        dn_sc = carve(2 * 8).rearrange("p (b c) -> p b c", b=2)
        neg_half = carve(1)
        score_f = carve(1)
        out_f = carve(1)
        stats = carve(4 * 12).rearrange("p (b c) -> p b c", b=4)
        mv = carve(4 * 2).rearrange("p (b c) -> p b c", b=4)
        vpe = carve(4)
        rstd = carve(4)
        rs2 = carve(4)
        base = place["at"]

        w_q = carve(8192, F16).rearrange("p (s k n) -> p s k n", s=2, k=KD)
        w_k = carve(2048, F16).rearrange("p (s k n) -> p s k n", s=2, k=KD)
        w_v = carve(2048, F16).rearrange("p (s k n) -> p s k n", s=2, k=KD)
        w_o = carve(8192, F16).rearrange("p (s k n) -> p s k n", s=2, k=KD)
        XB = 3
        X_LOADS = [2, 1, 1]
        xin = carve(XB * D).rearrange("p (b n) -> p b n", b=XB)
        xnt = carve(4096, F16).rearrange("p (s k n) -> p s k n", s=2, k=KD)
        p32 = carve(PB * 1024, at=place["at"] - 4096).rearrange("p (b n) -> p b n", b=PB)
        qt_at = place["at"]
        qt = carve(2048, F16).rearrange("p (s b m n) -> p s b m n", s=2, b=2, m=2)
        qs_at = place["at"]
        q_s = carve(8192, F16).rearrange("p (h n) -> p h n", h=NH)
        k_s = carve(2048, F16).rearrange("p (g n) -> p g n", g=NKV)
        v_a = carve(TT * NKV * 33 // 2, F16).rearrange("p (t g d) -> p t g d", t=TT, g=NKV)
        v_b = carve(TT * NKV * 33 // 2, F16).rearrange("p (t g d) -> p t g d", t=TT, g=NKV)
        p_at = place["at"]
        xb = carve(D)
        x2t = carve(KD * P, F16).rearrange("p (s k n) -> p s k n", s=2, k=KD)
        p_hl = carve(PB * 1024, F16).rearrange("p (b s n) -> p b s n", b=PB, s=2)
        attn = carve(2 * D).rearrange("p (b n) -> p b n", b=2)
        at_t = carve(2 * KD * P, F16, at=qt_at).rearrange("p (b s k n) -> p b s k n", b=2, s=2, k=KD)
        xr_at = place["at"]
        xr = carve(2 * D).rearrange("p (b n) -> p b n", b=2)
        mask = carve(S // 2, BF16)
        mcol = carve(NH * TT).rearrange("p (t h) -> p t h", t=TT)
        mrow = carve(S, F16).rearrange("p (s n) -> p s n", s=2)
        wabs = carve(4)
        wall = carve(4)
        wpow = carve(4)
        wfac = carve(4)
        rsum = carve(2 * 2 * NREP).rearrange("p (b t d) -> p b t d", b=2, d=1)
        stage_q = carve(8192, at=qs_at).rearrange("p (k n) -> p k n", k=KD)
        stage_o = carve(8192, at=p_at).rearrange("p (k n) -> p k n", k=KD)
        stage_k = carve(2048, at=xr_at).rearrange("p (k n) -> p k n", k=KD)
        stage_v = carve(2048, at=qt_at).rearrange("p (k n) -> p k n", k=KD)
        place["at"] = base
        xt = carve(NB * 4096, F16).rearrange("p (t s k n) -> p t s k n", t=NB * TT, s=2, k=KD)
        xt_flat = carve(NB * 4096, F16, at=base).rearrange("p (t n) -> p t n", t=NB * TT)
        acc = carve(KD * NTOK).rearrange("p (o n) -> p o n", o=KD)
        gacc = carve(2 * NTOK).rearrange("p (b n) -> p b n", b=2)
        uacc = carve(NTOK)
        hid = carve(2 * NTOK, F16).rearrange("p (b s n) -> p b s n", b=2, s=2)
        RT = 3
        tmp = carve(RT * HALF).rearrange("p (r n) -> p r n", r=RT)
        int_gu = carve(2 * KD * P, I32)
        int_d = carve(D, I32)
        w_gu = carve(2 * KD * P, BF16).rearrange("p (b w k n) -> p b w k n", b=2, w=2, k=KD)
        w_d = carve(D, BF16).rearrange("p (b n) -> p b n", b=2)
        y_t = carve(4 * D, at=base).rearrange("p (b n) -> p b n", b=4)
        XF = 12
        x1_b = carve(XF * D, at=base + 4 * D).rearrange("p (b n) -> p b n", b=XF)

        psum = ctx.enter_context(nc.psum_tensor("psum", [P, 8 * 512], F32))
        job_slot = [psum[:, 0:1024], psum[:, 1024:2048]]
        wide_ps = psum[:, 2048:3072]
        pv_ps = [psum[:, 3072:3336], psum[:, 3584:3848]]
        ffn_slot = [psum[:, 1024 * s:1024 * s + 1024] for s in range(4)]

        def sem(name):
            return ctx.enter_context(nc.semaphore(name))

        ident_ready = sem("ident_ready")
        consts_ready = sem("consts_ready")
        settled = sem("settled")
        x_loaded = [sem(f"x_loaded{i}") for i in range(XB)]
        w_loaded = [sem(f"w_loaded{i}") for i in range(4)]
        s_loaded = sem("s_loaded")
        wabs_ready = sem("wabs_ready")
        wall_ready = sem("wall_ready")
        wfac_ready = sem("wfac_ready")
        whi_ready = sem("whi_ready")
        wlo_ready = sem("wlo_ready")
        dve_step = sem("dve_step")
        scales_ready = sem("scales_ready")
        var_ready = [sem(f"var_ready{i}") for i in range(2)]
        rstd_ready = [sem(f"rstd_ready{i}") for i in range(2)]
        xn_ready = [sem(f"xn_ready{i}") for i in range(2)]
        slot_full = [sem(f"slot_full{i}") for i in range(2)]
        slot_free = [sem(f"slot_free{i}") for i in range(2)]
        hi_ready = sem("hi_ready")
        ks_stacked = sem("ks_stacked")
        qs_stacked = [sem(f"qs_stacked{i}") for i in range(2)]
        wide_full = sem("wide_full")
        wide_free = sem("wide_free")
        mrow_loaded = sem("mrow_loaded")
        p_masked = sem("p_masked")
        phi_ready = sem("phi_ready")
        plo_ready = sem("plo_ready")
        pv_done = sem("pv_done")
        pv_free = sem("pv_free")
        xr_loaded = [sem(f"xr_loaded{i}") for i in range(2)]
        x1_ready = sem("x1_ready")
        x1_stored = [sem(f"x1_stored{i}") for i in range(2)]
        x2t_stored = sem("x2t_stored")
        xt_loaded = [sem(f"xt_loaded{b}") for b in range(NB)]
        acc_zero = sem("acc_zero")
        unit_full = [sem(f"unit_full{s}") for s in range(4)]
        unit_free = [sem(f"unit_free{s}") for s in range(4)]
        gu_loaded = sem("gu_loaded")
        d_loaded = sem("d_loaded")
        gu_conv = sem("gu_conv")
        d_conv = sem("d_conv")
        gusc_ready = sem("gusc_ready")
        dnsc_ready = sem("dnsc_ready")
        silu_done = sem("silu_done")
        h32_ready = sem("h32_ready")
        hhi_ready = sem("hhi_ready")
        h_ready = sem("h_ready")
        tmp_free = sem("tmp_free")
        fvar_ready = sem("fvar_ready")
        frstd_ready = sem("frstd_ready")
        fnmr_ready = sem("fnmr_ready")
        x1b_loaded = [sem(f"x1b_loaded{i}") for i in range(XF)]
        out_ready = [sem(f"out_ready{i}") for i in range(2)]
        out_stored = [sem(f"out_stored{i}") for i in range(4)]

        def settle(eng):
            eng.sem_inc(settled, 1)

        def wait(eng, s, value):
            if not isinstance(value, int):
                eng.wait_ge(s, value)
                if eng is nc.sync:
                    settle(eng)
            elif value > 0:
                eng.wait_ge(s, value)

        def max_jobs(m):
            return [("MA", 4 * m), ("MA", 4 * m + 1), ("MB", 2 * m),
                    ("MA", 4 * m + 2), ("MA", 4 * m + 3), ("MB", 2 * m + 1)]

        TAIL = [("T1", 0), ("R", 8), ("T2", 3), ("R", 9), ("T1", 1), ("LN", 3)]
        TAIL += [("R", 10), ("LX", 3)] + [("WP", 24 + i) for i in range(4)] + [("T1", 2), ("R", 11), ("T1", 3)]
        TAIL += [("WP", 28 + i) for i in range(4)] + [("WO", 3), ("R", 12), ("T3", 2), ("R", 13)]
        STACKED = 21
        PACE = (1, 2, 1, 2)
        LATE_BEFORE = 3
        LATE_STEPS = [("R", 4 * (TT - 1) + 2), ("R", 4 * (TT - 1) + 3), ("T3", TT - 1)]
        events = []
        maxima_left = [(8 * (m // 2) + STACKED, job) for m in range(8) for job in max_jobs(m)]
        proj = [("K", 0), ("K", 1)] + [("Q", m) for m in range(8)] + [("V", 0), ("V", 1)]
        for n in range(4 * len(proj)):
            events += [("PP", (proj[n // 4], n % 4))]
            if n % 4 == 3:
                events += [proj[n // 4]]
            if n in (4, 6, 8):
                events += [LATE_STEPS[(n - 4) // 2]]
            for _ in range(PACE[n % 4]):
                if maxima_left and maxima_left[0][0] <= n:
                    events += [maxima_left.pop(0)[1]]
        late = [job for _, job in maxima_left if job[1] >= (24 if job[0] == "MA" else 12)]
        late = late[len(late) % 2:]
        events += [job for _, job in maxima_left if job not in late] + [("MT", 0)]
        behind = {14: [("T2", 0)], 23: [("T2", 1)], 32: [("T2", 2)],
                  15: [("LN", 0), ("LN", 1)], 16: [("LX", 0), ("LX", 1)], 19: [("LN", 2)], 20: [("LX", 2)]}
        for t, u in ((0, 15), (1, 24), (2, 34)):
            for i in range(8):
                behind.setdefault(u + (i if t < 2 else i * 3 // 4), []).append(("WP", 8 * t + i))
            behind[u + 7 if t < 2 else u + 5].append(("WO", t))
            if u + 12 < NS:
                for i in range(4):
                    behind.setdefault(u + 7 + i, []).append(("R", 4 * t + i))
                behind.setdefault(u + 12, []).append(("T3", t))
        LATE_BEFORE += (len(late) - LATE_BEFORE) % 2
        events += late[0:LATE_BEFORE]
        first_late = late[LATE_BEFORE:]
        late = set(first_late)
        for n, job in enumerate(first_late):
            behind.setdefault(n // 2, []).insert(0, job)
        n_last = (len(first_late) - 1) // 2
        assert n_last + 1 < LATE_UNIT - 1
        behind.setdefault(n_last + 1, []).append(("MT", 1))
        for u in range(NS):
            events += [("S", u)] + ([("PV", u - LAG)] if u >= LAG else []) + behind.get(u, [])
        events += [("END", 0)] + [("PV", NS - LAG + i) for i in range(LAG)]
        events += [("END", 1)] + TAIL
        epilogue = LATE_STEPS
        prologue = [("LN", 0), ("LN", 1), ("T1", 0), ("LN", 2), ("T1", 1), ("LN", 3), ("T1", 2), ("T1", 3)]
        SLOT_KINDS = ("T1", "K", "MA", "MB", "S", "T2", "T3")
        SPLIT = ("T1", "K", "V", "Q", "T2", "T3")
        WIDE = {job: n for n, job in enumerate([e for e in events if e[0] in ("Q", "V", "MT", "WO") or e in late])}
        NW = len(WIDE)

        def wide_bank(job):
            return wide_ps[:, 512 * (WIDE[job] % 2):512 * (WIDE[job] % 2) + 512]

        def wide_wait(eng, b, job):
            n = WIDE[job]
            alone = job[0] == "WO" or job in late or job == ("MT", 1) or n == 0
            wait(eng, wide_free, b * NW + (n if alone else n - 1))

        def head_range(i):
            return (0, NREP * EARLY) if i == 0 else (NREP * EARLY, NH)

        def is_first(b):
            return isinstance(b, int) and b == 0

        def is_last(b):
            return isinstance(b, int) and b == NB - 1

        def events_of(b):
            return [e for e in events if not (is_last(b) and e[0] in ("T1", "LN", "LX"))
                    and not (is_first(b) and e in LATE_STEPS)]

        def owner(b, ev):
            return b + 1 if ev[0] in ("T1", "LN", "LX") else b - 1 if ev in LATE_STEPS else b

        class Numbers:

            def __init__(self, kinds):
                lists = [[e for e in events_of(b) if e[0] in kinds and e not in late] for b in (0, None, NB - 1)]
                self.first, self.middle, self.last = [{e: n for n, e in enumerate(es)} for es in lists]
                self.start = TT + len(self.first)
                self.per = len(self.middle)

            def of(self, b, job):
                if job[0] == "T1":
                    return (0, job[1]) if is_first(b) else self.in_list(b - 1, job)
                if job in LATE_STEPS:
                    return self.in_list(b + 1, job)
                return self.in_list(b, job)

            def in_list(self, b, job):
                if isinstance(b, int) and b == 0:
                    return 0, TT + self.first[job]
                if isinstance(b, int) and b == NB:
                    return NB - 2, self.start + len(self.last) + [e for e in epilogue if e[0] == "T3"].index(job)
                table = self.last if is_last(b) else self.middle
                return b - 1, self.start + table[job]

        SLOTS, HIS = Numbers(SLOT_KINDS), Numbers(SPLIT + ("MT",))
        assert SLOTS.per % 2 == 0

        def slot_number(b, job):
            before, n = SLOTS.of(b, job)
            return n % 2, before * (SLOTS.per // 2) + n // 2

        def slot(b, job):
            return job_slot[slot_number(b, job)[0]]

        def wait_full(eng, b, job):
            s, n = slot_number(b, job)
            wait(eng, slot_full[s], n + 1)

        def wait_free(eng, b, job):
            s, n = slot_number(b, job)
            wait(eng, slot_free[s], n + 1)

        def full(ins, b, job):
            ins.then_inc(slot_full[slot_number(b, job)[0]], 1)

        def free(ins, b, job):
            ins.then_inc(slot_free[slot_number(b, job)[0]], 1)

        def split_views(b, job):
            kind, i = job
            if kind == "V":
                src = wide_bank(job).rearrange("p (t g d) -> p t g d", t=2, g=NKV)
                return src, v_a[:, 2 * i:2 * i + 2, :, 0:HD], v_b[:, 2 * i:2 * i + 2, :, 0:HD]
            if kind == "K":
                return slot(b, job)[:, 0:S], qt[:, 0, 1, i, :], qt[:, 1, 1, i, :]
            if kind == "Q":
                u = i // 2
                return wide_bank(job), qt[:, 0, u % 2, i % 2, :], qt[:, 1, u % 2, i % 2, :]
            ps = slot(b, job)
            src = ps.rearrange("p (k n) -> p k n", k=KD)
            if kind == "T1":
                return src, xnt[:, 0, :, P * i:P * i + P], xnt[:, 1, :, P * i:P * i + P]
            dst = at_t[:, i % 2] if kind == "T2" else x2t
            return src, dst[:, 0], dst[:, 1]

        def max_parts(job):
            kind, i = job
            if kind == "MA":
                return [(i, 3, 0), (i, 2, 512), (i, 0, 896)]
            return [(2 * i, 1, 0), (2 * i + 1, 1, 256)]

        GU = 4 * KD
        DN = 2 * KD
        AT_H, AT_HI, AT_LO = [1, 2], [3, 4], [4, 6]
        CARRY = 4
        order_zero = [("g", j + c) for c in range(2) for j in range(0, GU, 2)]
        order, n_d = [], 0
        for j in range(GU):
            order.append(("g", j))
            if j % 2 and j < 2 * CARRY:
                order.append(("c", DN - CARRY + j // 2))
            while n_d < (DN - CARRY) * (j - 2 * CARRY + 1) // (GU - 2 * CARRY):
                order.append(("d", n_d))
                n_d += 1
        assert n_d == DN - CARRY
        order_one = [u for u in order if u[0] != "c"]
        order_last = [("c", j) for j in range(DN - CARRY, DN)] + [("d", 2 * (j % KD) + j // KD) for j in range(DN)]
        DVE_D = [9]
        DVE_LAST = list(range(DN - CARRY))

        def dve_adds(n, u):
            if isinstance(n, int) and n == NT:
                return u[0] == "d" and u[1] in DVE_LAST
            return u[1] in DVE_D

        NPD = DN - len(DVE_D)
        NPC = len([j for j in range(DN - CARRY, DN) if j not in DVE_D])
        assert NPD % RT == 0 and (GU + DN) % 4 == 0 and GU % 4 == 0 and CARRY % 4 == 0

        def unit_list(n):
            if isinstance(n, int) and n < 2:
                units, before = (order_zero, 0) if n == 0 else (order_one, GU // 4)
            else:
                units = order_last if isinstance(n, int) and n == NT else order
                before = n * ((GU + DN) // 4) - (DN + CARRY) // 4
            return {u: (pos % 4, before + pos // 4) for pos, u in enumerate(units)}

        def pool_units(n):
            us = [u for u in unit_list(n) if u[0] != "g" and not dve_adds(n, u)]
            at = 0 if isinstance(n, int) and n == 1 else (n - 1) * NPD - NPC
            return [(u, at + q, (q - (0 if isinstance(n, int) and n == 1 else NPC)) % RT) for q, u in enumerate(us)]

        def gu_parts(j):
            return j // 16, (j % 16) // 2, j % 2

        def unit_done(eng, units, u):
            s, c = units[u]
            eng.wait_ge(unit_free[s], c + 1)

        def unit_filled(eng, units, u):
            s, c = units[u]
            wait(eng, unit_full[s], c + 1)

        def over_tiles(eng, one_tile):
            one_tile(0, 0)
            one_tile(1, 1)
            with eng.Fori(0, (NT - 4) // 2) as i:
                one_tile(i * 2 + 2, 0)
                one_tile(i * 2 + 3, 1)
            one_tile(NT - 2, 0)
            one_tile(NT - 1, 1)

        def over_batches(eng, one_batch):
            one_batch(0)
            with eng.Fori(1, NB - 1) as b:
                one_batch(b)
            one_batch(NB - 1)

        NF = NTOK // P
        F0 = NT * (GU + DN) // 4

        def add_x1(eng, f):
            eng.wait_ge(unit_free[f % 4], F0 + f // 4 + 1)
            eng.wait_ge(x1b_loaded[f % XF], 16 * (f // XF + 1))
            eng.tensor_tensor(y_t[:, f % 4, :], y_t[:, f % 4, :], x1_b[:, f % XF, :],
                              ALU.add).then_inc(out_ready[f % 2], 1)

        WEIGHTS_BEHIND = {("K", 0): (2, [0]), ("K", 1): (2, [1, 2, 3]), ("Q", 2): (3, [0, 1]), ("Q", 3): (3, [2, 3])}
        W_PARTS = [0, 1, 2, 6, 10]

        block = ctx.enter_context(nc.Block())

        @block.sync
        def _(sp):
            x_tiles = x.rearrange("b (t p) n -> b t p n", p=P)

            def load_x(b, t):
                sp.dma_start(xin[:, t % XB, :], x_tiles[b, t]).then_inc(x_loaded[t % XB], 16)

            sp.dma_start(xin[:, 0, :], x_tiles[0, 0]).then_inc(x_loaded[0], 16)
            sp.dma_start(xin[:, 1, :], x_tiles[0, 1]).then_inc(x_loaded[1], 16)
            for n, (dst, src) in enumerate(((stage_k, wk), (stage_v, wv), (stage_q, wq), (stage_o, wo))):
                sp.dma_start(dst, src.rearrange("(k p) n -> p k n", p=P)).then_inc(w_loaded[n], 16)
                if n == 1:
                    load_x(0, 2)
                    wait_full(sp, 0, ("T1", 0))
                    load_x(0, 3)
            sp.dma_start(all_scales[:, :, 0:24], scales.rearrange("n p c -> p n c")).then_inc(s_loaded, 16)

            def stack_queries(b, u):
                if u == 0:
                    if is_first(b):
                        wait(sp, wlo_ready, W_PARTS[3])
                wait(sp, wide_free, b * NW + WIDE[("Q", 2 * u + 1)] + 1)
                for c in range(3):
                    rows = q_s[HD * c:HD * c + HD, 8 * u:8 * u + 8, :].rearrange("p (m r) n -> p m r n", r=NREP)
                    for r in range(NREP):
                        sp.dma_start(rows[:, :, r, :], qt[HD * r:HD * r + HD, 1 if c == 1 else 0, u % 2, :, :])\
                            .then_inc(qs_stacked[u % 2], 16)

            def load_residual(b, t):
                if is_first(b) and t < 2:
                    sp.wait_ge(wlo_ready, W_PARTS[4])
                elif t < 2:
                    wait(sp, x1_stored[t], b * 32)
                else:
                    wait(sp, x1_stored[t % 2], b * 32 + 16)
                    wait(sp, xn_ready[1], b * TT + t - 1)
                sp.dma_start(xr[:, t % 2, :], x_tiles[b, t]).then_inc(xr_loaded[t % 2], 16)

            def store_x1(b, t):
                wait(sp, x1_ready, b * TT + t + 1)
                sp.dma_start(x1_scr[b, t], xr[:, t % 2, :]).then_inc(x1_stored[t % 2], 16)

            def store_x2t(b, t):
                wait_free(sp, b, ("T3", t))
                sp.dma_start(xt_scr[b, t], x2t.rearrange("p s k n -> p (s k n)")).then_inc(x2t_stored, 16)

            def batch(b):
                if not is_last(b):
                    wait_full(sp, b, ("T1", 3))
                    for t in range(XB):
                        load_x(b + 1, t)
                wait_free(sp, b, ("K", 1))
                for c in range(3):
                    rows = k_s[HD * c:HD * c + HD, :, :].rearrange("p (m r) n -> p m r n", r=NREP)
                    for r in range(NREP):
                        sp.dma_start(rows[:, :, r, :], qt[HD * r:HD * r + HD, 1 if c == 2 else 0, 1, :, :])\
                            .then_inc(ks_stacked, 16)
                for u in range(NU):
                    stack_queries(b, u)
                    if u == 0 and not is_first(b):
                        store_x1(b - 1, TT - 1)
                        store_x2t(b - 1, TT - 1)
                        load_residual(b, 1)
                for m in range(2):
                    first, end = head_range(m)
                    wait(sp, wide_free, b * NW + WIDE[("MT", m)] + 1)
                    for i in range(2):
                        sp.dma_start(q_s[3 * HD + i:3 * HD + i + 1, first:end, :], mrow[0:end - first, i, :])\
                            .then_inc(mrow_loaded, 16)
                load_residual(b, 0)
                if is_first(b):
                    load_residual(b, 1)
                if is_last(b):
                    sp.wait_ge(wide_full, b * NW + WIDE[("V", 1)] + 1)
                    sp.wait_ge(x2t_stored, 16 * TT * b)
                    for i in range(b):
                        sp.dma_start(xt_flat[:, TT * i:TT * i + TT, :], xt_scr[i].rearrange("t p n -> p t n"))\
                            .then_inc(xt_loaded[i], 16)
                for t in range(TT - 1):
                    if t == 2 and not is_last(b):
                        wait_full(sp, b + 1, ("T1", 0))
                        load_x(b + 1, 3)
                    store_x1(b, t)
                    if t < 2:
                        load_residual(b, t + 2)
                    if is_last(b) and t == 2:
                        wait_full(sp, b, ("T2", 3))
                        sp.dma_start(int_gu, gu_t[0]).then_inc(gu_loaded, 16)
                        sp.dma_start(int_d, down_t[0]).then_inc(d_loaded, 16)
                    store_x2t(b, t)

            over_batches(sp, batch)
            store_x1(NB - 1, TT - 1)
            store_x2t(NB - 1, TT - 1)
            sp.wait_ge(x2t_stored, 16 * NB * TT)
            sp.dma_start(xt_flat[:, TT * (NB - 1):TT * NB, :], xt_scr[NB - 1].rearrange("t p n -> p t n"))\
                .then_inc(xt_loaded[NB - 1], 16)

            def tile(n, par):
                if isinstance(n, int) and n == NT - 1:
                    return
                wait(sp, gu_conv, n + 1)
                sp.dma_start(int_gu, gu_t[n + 1]).then_inc(gu_loaded, 16)
                wait(sp, d_conv, n + 1)
                sp.dma_start(int_d, down_t[n + 1]).then_inc(d_loaded, 16)

            over_tiles(sp, tile)

            last = unit_list(NT - 1)
            for u in order[-4:]:
                unit_filled(sp, last, u)
            def load_x1(f):
                sp.dma_start(x1_b[:, f % XF, :], x1_scr[f // TT, f % TT]).then_inc(x1b_loaded[f % XF], 16)

            for f in range(XF):
                load_x1(f)
            for f in range(NF):
                wait(sp, out_ready[f % 2], f // 2 + 1)
                sp.dma_start(out[f * P:f * P + P, :], y_t[:, f % 4, :]).then_inc(out_stored[f % 4], 16)
                if f + XF < NF:
                    load_x1(f + XF)
            for i in range(4):
                wait(sp, out_stored[i], 16 * NF // 4)

        @block.gpsimd
        def _(pool):
            pool.memset(ident, 0.0).then_inc(ident_ready, 1)
            pool.wait_ge(ident_ready, 1)
            pool.affine_select(out=ident, in_=ident, compare_op=ALU.not_equal, fill=1.0, base=0,
                               pattern=[[-1, P]], channel_multiplier=1).then_inc(ident_ready, 1)
            pool.memset(neg_half, -0.5).then_inc(consts_ready, 1)
            pool.memset(mask, 0.0).then_inc(consts_ready, 1)
            pool.wait_ge(consts_ready, 2)
            tri = mask[:, S - P:S]
            pool.affine_select(out=tri, in_=tri, compare_op=ALU.is_ge, fill=NEG, base=0,
                               pattern=[[-1, P]], channel_multiplier=1).then_inc(consts_ready, 1)
            pool.memset(v_a.rearrange("p t g d -> p (t g d)"), 1.0).then_inc(consts_ready, 1)
            pool.memset(v_b.rearrange("p t g d -> p (t g d)"), 0.0).then_inc(consts_ready, 1)
            pool.wait_ge(consts_ready, 5)
            unit_rows = k_s[3 * HD:SOFTMAX_ROWS, :, :].rearrange("p g n -> p (g n)")
            pool.memset(unit_rows, MAX_UNIT).then_inc(consts_ready, 1)
            pool.wait_ge(consts_ready, 6)

            def power(which, count, i):
                pool.wait_ge(var_ready[which], count)
                pool.tensor_tensor(rstd[:, i:i + 1], vpe[:, i:i + 1], neg_half, ALU.pow).then_inc(rstd_ready[which], 1)

            def weight_max(n):
                pool.wait_ge(wabs_ready, n + 1)
                pool.partition_all_reduce(wall[:, n:n + 1], wabs[:, n:n + 1], P,
                                          bass.bass_isa.ReduceOp.max).then_inc(wall_ready, 1)

            for n in range(TT):
                power(0, n + 1, n % 2)
                if n < 2:
                    weight_max(n)
            weight_max(2)
            weight_max(3)

            def batch(b):
                for ev in events_of(b):
                    kind, i = ev
                    if kind == "LN":
                        power(0, (b + 1) * TT + i + 1, i % 2)
                    elif kind == "R" and i % 2 == 0:
                        power(1, owner(b, ev) * 2 * TT + i // 2 + 1, 2 + i % 4 // 2)
                    elif kind == "S" and MASKED[i]:
                        wait_free(pool, b, ev)
                        settle(pool)
                        for x, (t, _, j) in enumerate(S_UNITS[i]):
                            if j == t:
                                d = p32[:, i % PB, 512 * x:512 * x + 512].rearrange("p (h n) -> p h n", h=NREP)
                                ins = pool.affine_select(out=d, in_=d, compare_op=ALU.is_ge, fill=0.0, base=0,
                                                         pattern=[[0, NREP], [1, P]], channel_multiplier=-1)
                        ins.then_inc(p_masked, 1)

            over_batches(pool, batch)
            power(1, NB * 2 * TT, 3)
            pool.sem_inc(tmp_free, RT)
            pool.wait_ge(wide_full, NB * NW)
            pool.memset(acc.rearrange("p o n -> p (o n)"), 0.0).then_inc(acc_zero, 1)
            pool.wait_ge(acc_zero, 1)

            def tile(n, par):
                units = unit_list(n)
                for u, number, buf in pool_units(n):
                    o, c = u[1] // 2, u[1] % 2
                    unit_done(pool, units, u)
                    pool.wait_ge(tmp_free, RT + number - 1)
                    a = acc[:, o, c * HALF:c * HALF + HALF]
                    pool.tensor_tensor(a, tmp[:, buf, :], a, ALU.add).then_inc(tmp_free, 1)

            over_tiles(pool, tile)
            tile(NT, 0)
            for f in range(NF):
                pool.wait_ge(fvar_ready, f + 1)
                pool.tensor_tensor(rstd[:, f % 4:f % 4 + 1], vpe[:, f % 4:f % 4 + 1], neg_half,
                                   ALU.pow).then_inc(frstd_ready, 1)
                if f >= 2 and f % 2:
                    add_x1(pool, f - 2)
            add_x1(pool, NF - 1)

        @block.scalar
        def _(act):
            w_hi = [w_k[:, 0], w_v[:, 0], w_q[:, 0], w_o[:, 0]]
            stages = [stage_k, stage_v, stage_q, stage_o]

            def weight_hi(n, part):
                act.wait_ge(wfac_ready, n + 1)
                cols = slice(256 * part, 256 * part + 256)
                act.activation(w_hi[n][:, :, cols], stages[n][:, :, cols], ACT.Copy,
                               scale=wfac[:, n:n + 1]).then_inc(whi_ready, 1)

            def probabilities_hi(b, u):
                if MASKED[u]:
                    act.wait_ge(p_masked, b * NM + sum(MASKED[0:u + 1]))
                else:
                    wait_free(act, b, ("S", u))
                wait(act, pv_done, b * NS + u - PB + 1)
                act.activation(p_hl[:, u % PB, 0, :], p32[:, u % PB, :], ACT.Copy).then_inc(phi_ready, 1)

            def split_hi(b, ev):
                kind, i = ev
                if kind == "K" and i == 0:
                    wait(act, qs_stacked[1], b * 384)
                    if is_first(b):
                        act.wait_ge(wlo_ready, 2)
                elif kind == "Q" and i % 2 == 0:
                    if i == 0:
                        wait(act, qs_stacked[0], b * 384)
                    elif i == 2:
                        act.wait_ge(ks_stacked, (b + 1) * 192)
                    else:
                        act.wait_ge(qs_stacked[i // 2 % 2], b * 384 + 192)
                elif kind == "V" and is_first(b):
                    act.wait_ge(consts_ready, 6)
                elif kind == "T1":
                    wait(act, plo_ready, b * NS)
                elif kind == "T2" and i >= 2:
                    act.wait_ge(wide_full, b * NW + WIDE[("WO", i - 2)] + 1)
                elif kind == "T3":
                    wait(act, x2t_stored, b * TT * 16 + i * 16)
                if ev in WIDE:
                    act.wait_ge(wide_full, b * NW + WIDE[ev] + 1)
                else:
                    wait_full(act, b, ev)
                src, hi, _ = split_views(b, ev)
                act.activation(hi, src, ACT.Copy).then_inc(hi_ready, 1)

            def batch(b):
                for ev in events_of(b):
                    kind, i = ev
                    if kind in SPLIT:
                        split_hi(owner(b, ev), ev)
                        if is_first(b) and ev in WEIGHTS_BEHIND:
                            n, parts = WEIGHTS_BEHIND[ev]
                            for part in parts:
                                weight_hi(n, part)
                    elif kind == "S":
                        if is_first(b) and i == 0:
                            act.wait_ge(wlo_ready, W_PARTS[4])
                            act.wait_ge(scales_ready, 1)
                        wait_full(act, b, ev)
                        wait(act, plo_ready, b * NS + i - PB + 1)
                        free(act.activation(p32[:, i % PB, :], slot(b, ev), ACT.Exp, scale=score_f[:, 0:1]), b, ev)
                        if i >= 1:
                            probabilities_hi(b, i - 1)
                    elif ev == ("END", 0):
                        probabilities_hi(b, NS - 1)
                    elif kind == "MT":
                        act.wait_ge(wide_full, b * NW + WIDE[ev] + 1)
                        wait(act, mrow_loaded, b * 64 + 32 * i)
                        first, end = head_range(i)
                        act.activation(mrow[0:end - first, 0, :], wide_bank(ev)[0:end - first, :], ACT.Copy,
                                       scale=-1.0 / MAX_UNIT).then_inc(hi_ready, 1)

            weight_hi(0, 0)
            weight_hi(1, 0)
            for ev in prologue:
                if ev[0] == "T1":
                    split_hi(0, ev)
            over_batches(act, batch)

            def convert_gu(n, par):
                act.wait_ge(gu_loaded, (n + 1) * 16)
                act.activation(w_gu[:, par].rearrange("p w k n -> p (w k n)"), int_gu, ACT.Copy).then_inc(gu_conv, 1)

            def convert_d(n, par):
                act.wait_ge(d_loaded, (n + 1) * 16)
                act.wait_ge(gusc_ready, n + 1)
                act.activation(w_d[:, par, :], int_d, ACT.Copy, scale=gu_sc[:, par, 24:25]).then_inc(d_conv, 1)

            act.wait_ge(x1_stored[0], 32 * NB)
            convert_gu(0, 0)
            split_hi(NB - 1, ("T3", TT - 1))
            act.wait_ge(x1_stored[1], 32 * NB)

            def down_unit(par, units, u, number, buf):
                o = u[1] // 2
                unit_filled(act, units, u)
                act.wait_ge(tmp_free, number + 1)
                act.activation(tmp[:, buf, :], ffn_slot[units[u][0]], ACT.Copy,
                               scale=dn_sc[:, par if u[0] == "c" else 1 - par, o:o + 1])\
                    .then_inc(unit_free[units[u][0]], 1)

            def tile(n, par):
                units = unit_list(n)
                down = {u: (number, buf) for u, number, buf in pool_units(n)}
                seen_d = False
                for u in units:
                    kind, j = u
                    if kind == "g":
                        w, g, c = gu_parts(j)
                        if j in AT_HI and not (isinstance(n, int) and n == 0):
                            hidden_hi(n - 1, 1 - par, AT_HI.index(j))
                        if g == 0:
                            unit_filled(act, units, u)
                            act.wait_ge(gusc_ready, n + 1)
                            if w == 0:
                                dst = gacc[:, par, c * HALF:c * HALF + HALF]
                            else:
                                wait(act, h_ready, n * 2)
                                dst = uacc[:, c * HALF:c * HALF + HALF]
                            act.activation(dst, ffn_slot[units[u][0]], ACT.Copy,
                                           scale=gu_sc[:, par, 8 * w:8 * w + 1]).then_inc(unit_free[units[u][0]], 1)
                        if j in (20, 21):
                            unit_done(act, units, ("g", j - 6))
                            ga = gacc[:, par, (j - 20) * HALF:(j - 20) * HALF + HALF]
                            act.activation(ga, ga, ACT.Silu).then_inc(silu_done, 1)
                        if j == 10:
                            if ("c", DN - 1) in units:
                                unit_filled(act, units, ("c", DN - 1))
                            convert_d(n, par)
                        if j == 25 and not (isinstance(n, int) and n == NT - 1):
                            convert_gu(n + 1, 1 - par)
                    elif u in down:
                        if kind == "d" and not seen_d:
                            act.wait_ge(dnsc_ready, n)
                            seen_d = True
                        down_unit(par, units, u, *down[u])

            def hidden_hi(m, par, c):
                act.wait_ge(h32_ready, m * 2 + c + 1)
                act.activation(hid[:, par, 0, c * HALF:c * HALF + HALF], uacc[:, c * HALF:c * HALF + HALF],
                               ACT.Copy).then_inc(hhi_ready, 1)

            over_tiles(act, tile)
            units = unit_list(NT)
            for c in range(2):
                hidden_hi(NT - 1, 1, c)
            act.wait_ge(dnsc_ready, NT)
            for u, number, buf in pool_units(NT):
                down_unit(0, units, u, number, buf)
            for f in range(NF):
                act.wait_ge(fnmr_ready, f + 1)
                if f >= 4:
                    act.wait_ge(out_stored[f % 4], 16 * (f // 4))
                act.activation(y_t[:, f % 4, :], ffn_slot[f % 4], ACT.Identity, bias=rs2[:, f % 4:f % 4 + 1],
                               scale=rstd[:, f % 4:f % 4 + 1]).then_inc(unit_free[f % 4], 1)

        @block.vector
        def _(dve):
            steps = {"base": 0, "n": 0}

            def link(ins):
                ins.then_inc(dve_step, 1)
                steps["n"] += 1
                dve.wait_ge(dve_step, steps["base"] + steps["n"])

            def variance(halves, i, fac=None):
                for k in range(2):
                    ins = dve.bn_stats(stats[:, i, 6 * k:6 * k + 6], halves[k])
                link(ins)
                settle(dve)
                link(dve.bn_aggr(mv[:, i, :], stats[:, i, :]))
                src = mv[:, i, 1:2]
                if fac is not None:
                    link(dve.tensor_scalar(vpe[:, i:i + 1], src, fac, fac, ALU.mult, ALU.mult))
                    src = vpe[:, i:i + 1]
                return dve.tensor_scalar(vpe[:, i:i + 1], src, EPS, None, ALU.add)

            w_stage = [stage_k, stage_v, stage_q, stage_o]
            w_hl = [w_k, w_v, w_q, w_o]

            def weight_factor(n):
                dve.wait_ge(w_loaded[n], 16)
                dve.tensor_reduce(wabs[:, n:n + 1], w_stage[n].rearrange("p k n -> p (k n)"), AX.X, ALU.max,
                                  apply_absolute_value=True).then_inc(wabs_ready, 1)
                dve.wait_ge(wall_ready, n + 1)
                power_of_two(wpow[:, n:n + 1], wall[:, n:n + 1])
                link(dve.tensor_scalar(wall[:, n:n + 1], wpow[:, n:n + 1], 0.5, None, ALU.mult))
                dve.reciprocal(wfac[:, n:n + 1], wall[:, n:n + 1]).then_inc(wfac_ready, 1)

            def power_of_two(dst, src):
                link(dve.tensor_scalar(dst, src, 1e-30, 1e30, ALU.max, ALU.min))
                link(dve.tensor_scalar(dst.bitcast(I32), dst.bitcast(I32), 0x7F800000, None, ALU.bitwise_and))

            def weight_lo(n, part):
                dve.wait_ge(whi_ready, W_PARTS[n] + part + 1)
                cols = slice(256 * part, 256 * part + 256)
                dve.scalar_tensor_tensor(out=w_hl[n][:, 1, :, cols], in0=w_stage[n][:, :, cols],
                                         scalar=wfac[:, n:n + 1], in1=w_hl[n][:, 0, :, cols],
                                         op0=ALU.mult, op1=ALU.subtract).then_inc(wlo_ready, 1)

            def scale_tables():
                dve.wait_ge(s_loaded, 16)
                link(dve.tensor_scalar(score_f, wpow[:, 0:1], wpow[:, 2:3], 0.25 * HD ** -0.5, ALU.mult, ALU.mult))
                link(dve.tensor_scalar(out_f, wpow[:, 1:2], wpow[:, 3:4], 0.25, ALU.mult, ALU.mult))
                inv = all_scales[:, :, 24:25]
                dve.wait_ge(wlo_ready, W_PARTS[4])
                low = stage_o[:, 0, 0:NT].rearrange("p (n c) -> p n c", c=1)
                link(dve.tensor_reduce(inv, all_scales[:, :, 0:8], AX.X, ALU.max, apply_absolute_value=True))
                link(dve.tensor_reduce(low, all_scales[:, :, 8:16], AX.X, ALU.max, apply_absolute_value=True))
                link(dve.tensor_tensor(inv, inv, low, ALU.mult))
                power_of_two(inv, inv)
                link(dve.tensor_scalar(inv, inv, 4096.0, None, ALU.mult))
                link(dve.reciprocal(low, inv))
                up = all_scales[:, :, 8:16]
                dve.tensor_tensor(up, up, low.broadcast_to([P, NT, 8]), ALU.mult).then_inc(scales_ready, 1)

            def input_variance(b, t):
                dve.wait_ge(x_loaded[t % XB], (b * X_LOADS[t % XB] + t // XB + 1) * 16)
                tile = xin[:, t % XB, :]
                variance([tile[:, 0:512], tile[:, 512:1024]], t % 2).then_inc(var_ready[0], 1)

            def input_normal(b, t):
                tile = xin[:, t % XB, :]
                dve.wait_ge(rstd_ready[0], b * TT + t + 1)
                dve.tensor_scalar(tile, tile, mv[:, t % 2, 0:1], rstd[:, t % 2:t % 2 + 1], ALU.subtract,
                                  ALU.mult).then_inc(xn_ready[0], 1)

            def hi_written(b, ev):
                before, n = HIS.of(b, ev)
                dve.wait_ge(hi_ready, before * HIS.per + n + 1)

            def split_lo(b, ev):
                hi_written(b, ev)
                src, hi, lo = split_views(b, ev)
                ins = dve.tensor_tensor(lo, src, hi, ALU.subtract)
                if ev in WIDE:
                    ins.then_inc(wide_free, 1)
                else:
                    free(ins, b, ev)

            def maxima(b, ev):
                if ev in late:
                    wait(dve, wide_full, b * NW + WIDE[ev] + 1)
                else:
                    wait_full(dve, b, ev)
                settle(dve)
                for h, t, at in max_parts(ev):
                    n = P * (t + 1)
                    sc = (wide_ps if ev in late else slot(b, ev))[:, at:at + n]
                    ins = dve.tensor_tensor_reduce(
                        out=sc, in0=sc, in1=mask[:, S - n:S], scale=1.0, scalar=NEG, op0=ALU.add, op1=ALU.max,
                        accum_out=mcol[:, t, h:h + 1])
                if ev in late:
                    ins.then_inc(wide_free, 1)
                else:
                    free(ins, b, ev)

            def probabilities_lo(b, u):
                dve.wait_ge(phi_ready, b * NS + u + 1)
                dve.tensor_tensor(p_hl[:, u % PB, 1, :], p32[:, u % PB, :], p_hl[:, u % PB, 0, :],
                                  ALU.subtract).then_inc(plo_ready, 1)

            def normalise(b, u):
                t, g, j = S_UNITS[u][-1]
                if j < t or GROUP_NO[t, g] % 2 == 0:
                    return
                n = GROUP_NO[t, g] // 2
                dve.wait_ge(pv_done, b * NS + u + 1)
                o = pv_ps[n % 2].rearrange("p (h d) -> p h d", h=2 * NREP)
                wait(dve, pv_free, b * NG2 + n - 1)
                r = rsum[:, n % 2]
                link(dve.reciprocal(r, o[:, :, HD:HD + 1]))
                dve.tensor_tensor(attn[:, t % 2, P * (g - 1):P * g + P].rearrange("p (h d) -> p h d", h=2 * NREP),
                                  o[:, :, 0:HD], r.broadcast_to([P, 2 * NREP, HD]), ALU.mult).then_inc(pv_free, 1)

            def residual(b, t, step):
                y, r = wide_ps, xr[:, t % 2, :]
                if step == 0:
                    dve.wait_ge(wide_full, b * NW + WIDE[("WO", t)] + 1)
                    variance([y[:, 0:512], y[:, 512:1024]], 2, out_f).then_inc(var_ready[1], 1)
                elif step == 1:
                    dve.wait_ge(rstd_ready[1], b * 2 * TT + 2 * t + 1)
                    link(dve.tensor_scalar(rs2[:, 0:1], rstd[:, 2:3], out_f, None, ALU.mult))
                    dve.tensor_scalar(xb, y, mv[:, 2, 0:1], rs2[:, 0:1], ALU.subtract, ALU.mult).then_inc(wide_free, 1)
                elif step == 2:
                    dve.wait_ge(wide_free, b * NW + WIDE[("WO", t)] + 1)
                    dve.wait_ge(xr_loaded[t % 2], b * 32 + (t // 2 + 1) * 16)
                    dve.tensor_tensor(r, r, xb, ALU.add).then_inc(x1_ready, 1)
                    dve.wait_ge(x1_ready, b * TT + t + 1)
                    variance([r[:, 0:512], r[:, 512:1024]], 3).then_inc(var_ready[1], 1)
                else:
                    dve.wait_ge(rstd_ready[1], b * 2 * TT + 2 * t + 2)
                    dve.tensor_scalar(xb, r, mv[:, 3, 0:1], rstd[:, 3:4], ALU.subtract,
                                      ALU.mult).then_inc(xn_ready[1], 1)

            def attention_step(b, ev):
                kind, i = ev
                if kind in SPLIT:
                    split_lo(owner(b, ev), ev)
                    if is_first(b) and ev in WEIGHTS_BEHIND:
                        n, parts = WEIGHTS_BEHIND[ev]
                        for part in parts:
                            weight_lo(n, part)
                    if is_first(b) and ev == ("Q", 1):
                        weight_factor(3)
                    if is_first(b) and ev == ("Q", 3):
                        scale_tables()
                elif kind in ("MA", "MB"):
                    maxima(b, ev)
                elif kind == "S" and i >= 1:
                    probabilities_lo(b, i - 1)
                elif ev == ("END", 0):
                    probabilities_lo(b, NS - 1)
                elif ev == ("END", 1):
                    normalise(b, NS - 1)
                elif kind == "PV" and i >= 1:
                    normalise(b, i - 1)
                elif kind == "MT":
                    hi_written(b, ev)
                    first, end = head_range(i)
                    dve.scalar_tensor_tensor(out=mrow[0:end - first, 1, :], in0=wide_bank(ev)[0:end - first, :],
                                             scalar=-1.0 / MAX_UNIT, in1=mrow[0:end - first, 0, :], op0=ALU.mult,
                                             op1=ALU.subtract).then_inc(wide_free, 1)
                elif kind == "R":
                    residual(owner(b, ev), i // 4, i % 4)
                elif kind == "LN":
                    input_variance(b + 1, i)
                elif kind == "LX":
                    input_normal(b + 1, i)

            def batch(b):
                for ev in events_of(b):
                    attention_step(b, ev)

            dve.wait_ge(consts_ready, 3)
            for ev in prologue:
                if ev[0] == "LN":
                    input_variance(0, ev[1])
                    input_normal(0, ev[1])
                    if ev[1] < 2:
                        weight_factor(ev[1])
                        if ev[1] == 1:
                            weight_lo(0, 0)
                            weight_lo(1, 0)
                else:
                    split_lo(0, ev)
            weight_factor(2)
            batch(0)
            per, first_steps = TT * 2 + NG2 + TT * 6, steps["n"]
            with dve.Fori(1, NB - 1) as b:
                steps["base"], steps["n"] = b * per + (first_steps - per), 0
                batch(b)
                assert steps["n"] == per, steps["n"]
            steps["base"], steps["n"] = (NB - 2) * per + first_steps, 0
            batch(NB - 1)
            for ev in epilogue:
                attention_step(NB, ev)

            def tile(n, par):
                first = isinstance(n, int) and n == 0
                units = unit_list(n)
                if first:
                    dve.tensor_copy(gu_sc[:, 0, :], all_scales[:, 0, :]).then_inc(gusc_ready, 1)
                if isinstance(n, int) and n == 1:
                    dve.wait_ge(acc_zero, 1)
                for u in units:
                    kind, j = u
                    ps = ffn_slot[units[u][0]]
                    done = unit_free[units[u][0]]
                    if kind == "g":
                        w, g, c = gu_parts(j)
                        if j in AT_H and not first:
                            hidden(n - 1, 1 - par, unit_list(n - 1), AT_H.index(j))
                        if j in AT_LO and not first:
                            hidden_lo(n - 1, 1 - par, AT_LO.index(j))
                        if g > 0:
                            unit_filled(dve, units, u)
                            unit_done(dve, units, ("g", j - 2))
                            a = (gacc[:, par] if w == 0 else uacc)[:, c * HALF:c * HALF + HALF]
                            dve.scalar_tensor_tensor(out=a, in0=ps, scalar=gu_sc[:, par, 8 * w + g:8 * w + g + 1],
                                                     in1=a, op0=ALU.mult, op1=ALU.add).then_inc(done, 1)
                        if j == 12 and not (isinstance(n, int) and n == NT - 1):
                            wait(dve, d_conv, n)
                            dve.tensor_copy(gu_sc[:, 1 - par, :], all_scales[:, n + 1, :]).then_inc(gusc_ready, 1)
                    elif j in DVE_D:
                        down_unit(n, par, units, u)
                carried = [u for u in units if u[0] == "c" and u[1] not in DVE_D]
                if carried:
                    unit_done(dve, units, carried[-1])
                dve.tensor_copy(dn_sc[:, par, :], all_scales[:, n, 16:24]).then_inc(dnsc_ready, 1)

            def hidden(m, par, units, c):
                unit_done(dve, units, ("g", GU - 2 + c))
                dve.wait_ge(silu_done, m * 2 + c + 1)
                ua = uacc[:, c * HALF:c * HALF + HALF]
                dve.tensor_tensor(ua, ua, gacc[:, par, c * HALF:c * HALF + HALF], ALU.mult).then_inc(h32_ready, 1)

            def hidden_lo(m, par, c):
                dve.wait_ge(hhi_ready, m * 2 + c + 1)
                dve.tensor_tensor(hid[:, par, 1, c * HALF:c * HALF + HALF], uacc[:, c * HALF:c * HALF + HALF],
                                  hid[:, par, 0, c * HALF:c * HALF + HALF], ALU.subtract).then_inc(h_ready, 1)

            def down_unit(n, par, units, u):
                o, c = u[1] // 2, u[1] % 2
                unit_filled(dve, units, u)
                dve.wait_ge(dnsc_ready, n)
                a = acc[:, o, c * HALF:c * HALF + HALF]
                scale = dn_sc[:, par if u[0] == "c" else 1 - par, o:o + 1]
                dve.scalar_tensor_tensor(out=a, in0=ffn_slot[units[u][0]], scalar=scale, in1=a, op0=ALU.mult,
                                         op1=ALU.add).then_inc(unit_free[units[u][0]], 1)

            over_tiles(dve, tile)
            for c in range(2):
                hidden(NT - 1, 1, unit_list(NT - 1), c)
            for c in range(2):
                hidden_lo(NT - 1, 1, c)
            units = unit_list(NT)
            dve.wait_ge(tmp_free, RT + pool_units(NT - 1)[-1][1] + 1)
            for u in units:
                if dve_adds(NT, u):
                    down_unit(NT, 0, units, u)

            for f in range(NF + 2):
                if f < NF:
                    y = ffn_slot[f % 4]
                    dve.wait_ge(unit_full[f % 4], F0 + f // 4 + 1)
                    variance([y[:, 0:512], y[:, 512:1024]], f % 4).then_inc(fvar_ready, 1)
                if 1 <= f <= NF:
                    i = (f - 1) % 4
                    dve.wait_ge(frstd_ready, f)
                    dve.tensor_scalar(rs2[:, i:i + 1], mv[:, i, 0:1], rstd[:, i:i + 1], -1.0, ALU.mult,
                                      ALU.mult).then_inc(fnmr_ready, 1)
                if f >= 2 and f % 2 == 0:
                    add_x1(dve, f - 2)

        @block.tensor
        def _(pe):
            PAIRS = ((0, 0), (0, 1), (1, 0))

            def transposes(dst, src, n):
                for k in range(n):
                    ins = pe.transpose(dst(k), src(k), ident)
                return ins

            def enter(b, ev):
                s, n = slot_number(b, ev)
                wait(pe, slot_free[s], n)

            def projection(b, job, piece):
                kind, i = job
                dst = slot(b, job)[:, 0:S] if kind == "K" else wide_bank(job)
                if kind == "V":
                    t, ks = piece // 2, range(KD // 2 * (piece % 2), KD // 2 * (piece % 2) + KD // 2)
                    tok = P * (2 * i + t)
                    dst = dst[:, 256 * t:256 * t + 256]
                    terms = lambda a, c, k: (xnt[:, a, k, tok:tok + P], w_v[:, c, k, :])
                else:
                    w = w_k if kind == "K" else w_q
                    ks = range(KD // 4 * piece, KD // 4 * piece + KD // 4)
                    terms = lambda a, c, k: (w[:, a, k, P * i:P * i + P], xnt[:, c, k, :])
                for k in ks:
                    for m, (a, c) in enumerate(PAIRS):
                        lhs, rhs = terms(a, c, k)
                        ins = pe.matmul(dst, lhs, rhs, start=(k == 0 and m == 0), stop=(k == KD - 1 and m == 2))
                if piece == 3 and kind == "K":
                    full(ins, b, job)
                elif piece == 3:
                    ins.then_inc(wide_full, 1)

            def input_transposes(b, t):
                ev = ("T1", t)
                enter(b, ev)
                pe.wait_ge(xn_ready[0], b * TT + t + 1)
                full(transposes(lambda k: slot(b, ev)[:, P * k:P * k + P],
                                lambda k: xin[:, t % XB, P * k:P * k + P], KD), b, ev)

            def residual_transposes(b, t):
                ev = ("T3", t)
                enter(b, ev)
                wait(pe, xn_ready[1], b * TT + t + 1)
                full(transposes(lambda k: slot(b, ev)[:, P * k:P * k + P], lambda k: xb[:, P * k:P * k + P], KD), b, ev)

            def batch(b):
                for ev in events_of(b):
                    kind, i = ev
                    if kind == "T1":
                        input_transposes(b + 1, i)
                        continue
                    if kind == "T3":
                        residual_transposes(owner(b, ev), i)
                        continue
                    if ev in late:
                        wide_wait(pe, b, ev)
                    elif kind in SLOT_KINDS and kind != "K":
                        enter(b, ev)
                    if kind == "PP":
                        job, piece = i
                        if piece == 0:
                            if job[0] == "K":
                                enter(b, job)
                            else:
                                wide_wait(pe, b, job)
                            if job == ("K", 0):
                                wait_free(pe, b, ("T1", TT - 1))
                            if is_first(b) and job == ("K", 0):
                                pe.wait_ge(wlo_ready, 2)
                            if is_first(b) and job[0] == "Q" and job[1] % 2 == 0:
                                pe.wait_ge(wlo_ready, W_PARTS[2] + job[1] // 2 + 1)
                        projection(b, job, piece)
                    elif kind in ("MA", "MB"):
                        if kind == "MA" and i % 8 == 0:
                            u = i // 8
                            pe.wait_ge(ks_stacked, (b + 1) * 192)
                            pe.wait_ge(qs_stacked[u % 2], b * 384 + (u // 2 + 1) * 192)
                        for h, t, at in max_parts(ev):
                            n = P * (t + 1)
                            dst = (wide_ps if ev in late else slot(b, ev))[:, at:at + n]
                            ins = pe.matmul(dst, q_s[0:3 * HD, h, P * t:P * t + P],
                                            k_s[0:3 * HD, h // NREP, 0:n], start=True, stop=True)
                        if ev in late:
                            ins.then_inc(wide_full, 1)
                        else:
                            full(ins, b, ev)
                    elif kind == "MT":
                        wide_wait(pe, b, ev)
                        first, end = head_range(i)
                        if i == 0:
                            wait_free(pe, b, ("MB", end // 2 - 1))
                        transposes(lambda t: wide_bank(ev)[0:end - first, P * t:P * t + P],
                                   lambda t: mcol[:, t, first:end], TT).then_inc(wide_full, 1)
                    elif kind == "S":
                        if i in (0, LATE_UNIT):
                            pe.wait_ge(mrow_loaded, b * 64 + (32 if i == 0 else 64))
                        for x, (t, g, j) in enumerate(S_UNITS[i]):
                            ins = pe.matmul(slot(b, ev)[:, 512 * x:512 * x + 512],
                                            k_s[0:SOFTMAX_ROWS, g, P * j:P * j + P],
                                            q_s[0:SOFTMAX_ROWS, NREP * g:NREP * g + NREP, P * t:P * t + P],
                                            start=True, stop=True)
                        full(ins, b, ev)
                    elif kind == "PV":
                        pe.wait_ge(plo_ready, b * NS + i + 1)
                        for x, (t, g, j) in enumerate(S_UNITS[i]):
                            n, second = GROUP_NO[t, g] // 2, GROUP_NO[t, g] % 2
                            if j == 0 and not second:
                                wait(pe, pv_free, b * NG2 + n - 1)
                            for r in range(NREP):
                                at = 33 * (NREP * second + r)
                                dst = pv_ps[n % 2][:, at:at + 33]
                                cols = slice(512 * x + P * r, 512 * x + P * r + P)
                                hi, lo = p_hl[:, i % PB, 0, cols], p_hl[:, i % PB, 1, cols]
                                pe.matmul(dst, hi, v_a[:, j, g, :], start=(j + r + second == 0), stop=False,
                                          skip_group_check=True)
                                pe.matmul(dst, hi, v_b[:, j, g, :], start=False, stop=False, skip_group_check=True)
                                ins = pe.matmul(dst, lo, v_a[:, j, g, :], start=False,
                                                stop=(j == t and r == NREP - 1 and second == 1),
                                                skip_group_check=True)
                        ins.then_inc(pv_done, 1)
                    elif kind == "T2":
                        pe.wait_ge(pv_free, b * NG2 + GROUP_NO[i, NKV - 1] // 2 + 1)
                        full(transposes(lambda k: slot(b, ev)[:, P * k:P * k + P],
                                        lambda k: attn[:, i % 2, P * k:P * k + P], KD), b, ev)
                    elif kind == "WP":
                        t, m, k0 = i // 8, i % 8 // 4, i % 4 * 2
                        if i % 8 == 0:
                            wide_wait(pe, b, ("WO", t))
                            wait_free(pe, b, ("T2", t))
                        for k in (k0, k0 + 1):
                            for n, (a, c) in enumerate(PAIRS):
                                ins = pe.matmul(wide_ps[:, 512 * m:512 * m + 512], at_t[:, t % 2, a, k, :],
                                                w_o[:, c, k, 512 * m:512 * m + 512], start=(k == 0 and n == 0),
                                                stop=(k == KD - 1 and n == 2))
                        if i % 8 == 7:
                            ins.then_inc(wide_full, 1)

            pe.wait_ge(ident_ready, 2)
            for ev in prologue:
                if ev[0] == "T1":
                    input_transposes(0, ev[1])
            over_batches(pe, batch)
            residual_transposes(NB - 1, TT - 1)
            wait_free(pe, NB - 1, ("T3", TT - 2))
            wait_free(pe, NB - 1, ("T3", TT - 1))
            pe.wait_ge(wide_free, NB * NW)
            pe.wait_ge(pv_free, NB * NG2)

            def gu_unit(n, par, units, u):
                w, g, c = gu_parts(u[1])
                s, _ = units[u]
                for m in range(2):
                    b = 2 * c + m
                    for hl in range(2):
                        ins = pe.matmul(ffn_slot[s][:, S * m:S * m + S], w_gu[:, par, w, g, :],
                                        xt[:, TT * b:TT * b + TT, hl, g, :],
                                        start=(hl == 0), stop=(hl == 1))
                ins.then_inc(unit_full[s], 1)

            def down_unit(n, par, units, u):
                o, c = u[1] // 2, u[1] % 2
                dpar = par if u[0] == "c" else 1 - par
                s, _ = units[u]
                for m in range(2):
                    at = c * HALF + S * m
                    for hl in range(2):
                        ins = pe.matmul(ffn_slot[s][:, S * m:S * m + S], w_d[:, dpar, P * o:P * o + P],
                                        hid[:, dpar, hl, at:at + S], start=(hl == 0), stop=(hl == 1))
                ins.then_inc(unit_full[s], 1)

            def tile(n, par):
                units = unit_list(n)
                first_d = True
                for u in units:
                    s, before = units[u]
                    wait(pe, unit_free[s], before)
                    if u[0] == "g":
                        if u[1] == 0:
                            pe.wait_ge(gu_conv, n + 1)
                        if isinstance(n, int) and n == 0 and u[1] < 2:
                            pe.wait_ge(xt_loaded[2 * u[1]], 16)
                            pe.wait_ge(xt_loaded[2 * u[1] + 1], 16)
                        gu_unit(n, par, units, u)
                    else:
                        if u[0] == "d" and first_d:
                            pe.wait_ge(d_conv, n)
                            pe.wait_ge(h_ready, n * 2)
                            first_d = False
                        down_unit(n, par, units, u)

            over_tiles(pe, tile)
            tile(NT, NT % 2)
            lasts = unit_list(NT)
            half_pool = [[number for u, number, _ in pool_units(NT) if u[0] == "c" or u[1] % 2 <= c][-1]
                         for c in range(2)]
            half_dve = [[u for u in lasts if u[0] == "d" and u[1] % 2 == c and dve_adds(NT, u)][-1:] for c in range(2)]
            for f in range(NF):
                c = f // (NF // 2)
                if f % (NF // 2) == 0:
                    pe.wait_ge(tmp_free, RT + half_pool[c] + 1)
                    for u in half_dve[c]:
                        unit_done(pe, lasts, u)
                pe.wait_ge(unit_free[f % 4], F0 + f // 4)
                for k in range(KD):
                    ins = pe.transpose(ffn_slot[f % 4][:, P * k:P * k + P], acc[:, k, f * P:f * P + P], ident)
                ins.then_inc(unit_full[f % 4], 1)


def kernel(L0_attn_x, L0_attn_wq, L0_attn_wk, L0_attn_wv, L0_attn_wo, L0_ffn_gate_q, L0_ffn_gate_s,
           L0_ffn_up_q, L0_ffn_up_s, L0_ffn_down_q, L0_ffn_down_s):
    import numpy as np
    import concourse.bacc as bacc
    from concourse import mybir as mb
    from concourse.bass_utils import run_bass_kernel_spmd

    p = 128
    x = np.asarray(L0_attn_x)
    gate, up, down = (np.asarray(a) for a in (L0_ffn_gate_q, L0_ffn_up_q, L0_ffn_down_q))
    gate_s, up_s, down_s = (np.asarray(a) for a in (L0_ffn_gate_s, L0_ffn_up_s, L0_ffn_down_s))
    inter, width = gate.shape
    nt, kd = inter // p, width // p
    gu = np.stack([gate, up]).reshape(2, nt, p, kd, p).transpose(1, 4, 0, 3, 2).reshape(nt, p, 2 * kd * p)
    dn = down.reshape(width, nt, p).transpose(1, 2, 0)
    sc = np.concatenate([gate_s.reshape(nt, p, kd), up_s.reshape(nt, p, kd),
                         down_s.reshape(kd, p, nt).transpose(2, 1, 0)], axis=2)
    arrays = {"x": x, "wq": L0_attn_wq, "wk": L0_attn_wk, "wv": L0_attn_wv, "wo": L0_attn_wo,
              "gu_t": gu, "down_t": dn, "scales": sc}
    arrays = {k: np.ascontiguousarray(v) for k, v in arrays.items()}

    nc = bacc.Bacc("TRN2", target_bir_lowering=False, num_devices=1)
    aps = {k: nc.dram_tensor(f"in_{k}", v.shape, mb.dt.from_np(v.dtype), kind="ExternalInput").ap()
           for k, v in arrays.items()}
    out = nc.dram_tensor("out_0", (x.shape[0] * x.shape[1], x.shape[2]), mb.dt.float32, kind="ExternalOutput").ap()
    sandwich(nc, out=out, **aps)
    r = run_bass_kernel_spmd(nc, [{f"in_{k}": v for k, v in arrays.items()}], core_ids=[0])
    return r.results[0]["out_0"].reshape(x.shape)
```
